# Optimizing a Trainium2 kernel written in Bass

```python
import numpy as np
import jax
import jax.numpy as jnp

def _softmax(x, axis=-1):
    return jax.nn.softmax(x, axis=axis)

def _gelu(x):
    return jax.nn.gelu(x, approximate=True)

def _silu(x):
    return jax.nn.silu(x)

def _sigmoid(x):
    return jax.nn.sigmoid(x)

def _layernorm(x, axis=-1, eps=1e-05):
    m = jnp.mean(x, axis=axis, keepdims=True)
    v = jnp.var(x, axis=axis, keepdims=True)
    return (x - m) / jnp.sqrt(v + eps)

def _scatter_add(tgt, idx, src, axis=0):
    return tgt.at[idx].add(src)

def _segment_sum(src, seg, n):
    return jax.ops.segment_sum(src, seg, n)
kernel_name = 'mk_adj_resnorm_d4_adj_r2_27432d'

def setup_inputs(seed: int=0):
    np.random.seed(seed)
    _w = jnp.asarray

    def _rec_inputs():
        import jax
        import jax.numpy as jnp
        _gk = jax.random.key(seed)
        x = -0.0002928 + 1 * jax.random.normal(jax.random.fold_in(_gk, 1), (3327, 128), jnp.float32)
        _w = (1.0 + jnp.arange(3327, dtype=jnp.float32)) ** (-0.5)
        _w = _w / _w.mean()
        _pij = jnp.clip(0.00480914 * _w[:, None] * _w[None, :], 0.0, 1.0)
        _a = jax.random.uniform(jax.random.fold_in(_gk, 2), (3327, 3327)) < _pij
        _a = jnp.logical_or(_a, jnp.eye(3327, dtype=bool))
        _af = _a.astype(jnp.float32)
        _af = _af * jax.random.uniform(jax.random.fold_in(_gk, 3), (3327, 3327), jnp.float32, 0.05, 1)
        adj = _af
        return (x, adj)
    x, adj = _rec_inputs()

    def _L0_gnn_setup():
        import jax, jax.numpy as jnp
        import numpy as np
        N = 8192
        D = 128
        OUT = 128
        key = jax.random.key(seed)
        k1, k2, k3 = jax.random.split(key, 3)
        features = jax.random.normal(k1, (N, D), dtype=jnp.float32)
        adj = jax.random.uniform(k2, (N, N), dtype=jnp.float32)
        W = jax.random.normal(k3, (OUT, 2 * D), dtype=jnp.float32)
        return {'features': features, 'adj': adj, 'W': W}
    _L0_gnn_all = _L0_gnn_setup()
    _L0_gnn_in = {k: v for k, v in _L0_gnn_all.items() if k in ('W',)}
    del _L0_gnn_all

    def _L1_gnn_setup():
        import jax, jax.numpy as jnp
        import numpy as np
        N = 4096
        EMB = 128
        EDGE_P = 0.004
        LN_EPS = 1e-05

        def _layernorm(h, g, b):
            mu = jnp.mean(h, axis=-1, keepdims=True)
            var = jnp.mean(jnp.square(h - mu), axis=-1, keepdims=True)
            return (h - mu) * jax.lax.rsqrt(var + LN_EPS) * g + b
        key = jax.random.key(seed)
        ks = jax.random.split(key, 10)
        x = jax.random.normal(ks[0], (N, EMB), dtype=jnp.float32)
        adj = (jax.random.uniform(ks[1], (N, N)) < EDGE_P).astype(jnp.float32)
        adj = jnp.fill_diagonal(adj, 1.0, inplace=False)
        s = 1.0 / np.sqrt(EMB)
        W1 = jax.random.normal(ks[2], (EMB, EMB), dtype=jnp.float32) * s
        b1 = jax.random.normal(ks[3], (EMB,), dtype=jnp.float32) * s
        W2 = jax.random.normal(ks[4], (EMB, EMB), dtype=jnp.float32) * s
        b2 = jax.random.normal(ks[5], (EMB,), dtype=jnp.float32) * s
        W3 = jax.random.normal(ks[6], (EMB, EMB), dtype=jnp.float32) * s
        b3 = jax.random.normal(ks[7], (EMB,), dtype=jnp.float32) * s
        ones = jnp.ones((EMB,), jnp.float32)
        zeros = jnp.zeros((EMB,), jnp.float32)
        return {'x': x, 'adj': adj, 'W1': W1, 'b1': b1, 'W2': W2, 'b2': b2, 'W3': W3, 'b3': b3, 'g1': ones, 'be1': zeros, 'g2': ones, 'be2': zeros, 'g3': ones, 'be3': zeros}
    _L1_gnn_all = _L1_gnn_setup()
    _L1_gnn_in = {k: v for k, v in _L1_gnn_all.items() if k in ('W1', 'b1', 'W2', 'b2', 'W3', 'b3', 'g1', 'be1', 'g2', 'be2', 'g3', 'be3')}
    del _L1_gnn_all

    def _L2_gnn_setup():
        import jax, jax.numpy as jnp
        import numpy as np
        N = 4096
        F_IN = 128
        F_OUT = 128
        key = jax.random.key(seed)
        k1, k2, k3, k4 = jax.random.split(key, 4)
        return {'input': jax.random.normal(k1, (N, F_IN), dtype=jnp.float32), 'adj': jax.random.uniform(k2, (N, N), dtype=jnp.float32), 'weight': jax.random.normal(k3, (F_IN, F_OUT), dtype=jnp.float32) * (1.0 / np.sqrt(F_OUT)), 'bias': jax.random.normal(k4, (F_OUT,), dtype=jnp.float32) * (1.0 / np.sqrt(F_OUT))}
    _L2_gnn_all = _L2_gnn_setup()
    _L2_gnn_in = {k: v for k, v in _L2_gnn_all.items() if k in ('weight', 'bias')}
    del _L2_gnn_all

    def _L3_gnn_setup():
        import jax, jax.numpy as jnp
        import numpy as np
        N, H, HEADS = (2048, 128, 3)
        ALPHA = 0.2
        NEG_INF = -9000000000000000.0

        def _sign_adj(key, n, density):
            k1, k2 = jax.random.split(key)
            mask = jax.random.uniform(k1, (n, n)) < density
            sign = jnp.where(jax.random.uniform(k2, (n, n)) < 0.5, -1.0, 1.0)
            adj = jnp.where(mask, sign, 0.0).astype(jnp.float32)
            idx = jnp.arange(n)
            return adj.at[idx, idx].set(1.0)

        def _gru_cell(x, hstate, Wih, Whh, bih, bhh):
            gi = x @ Wih.T + bih
            gh = hstate @ Whh.T + bhh
            ir, iz, inn = jnp.split(gi, 3, axis=1)
            hr, hz, hn = jnp.split(gh, 3, axis=1)
            r = jax.nn.sigmoid(ir + hr)
            z = jax.nn.sigmoid(iz + hz)
            n = jnp.tanh(inn + r * hn)
            return (1.0 - z) * n + z * hstate

        def _gat_head(h, node_adj, edge_adj, W, a):
            hW = h @ W
            hp = (node_adj > 0).astype(hW.dtype) @ hW
            hm = (node_adj < 0).astype(hW.dtype) @ hW
            e_plus = jax.nn.leaky_relu(jnp.concatenate([hp, hm], axis=1) @ a, ALPHA)[:, 0]
            e_minus = jax.nn.leaky_relu(jnp.concatenate([hm, hp], axis=1) @ a, ALPHA)[:, 0]
            att = jnp.where(edge_adj > 0, e_plus[None, :], NEG_INF)
            att = jnp.where(edge_adj < 0, e_minus[None, :], att)
            att = jax.nn.softmax(att, axis=1)
            return att * edge_adj @ hW
        key = jax.random.key(seed)
        ks = jax.random.split(key, 16)
        std = 0.01
        gain = 1.414
        return {'h': jax.random.normal(ks[0], (N, H), jnp.float32), 'node_adj': _sign_adj(ks[1], N, 0.005), 'edge_adj': _sign_adj(ks[2], N, 0.005), 'gat_W': jax.random.normal(ks[3], (HEADS, H, H), jnp.float32) * (gain / np.sqrt(H, dtype=np.float32)), 'gat_a': jax.random.normal(ks[4], (HEADS, 2 * H, 1), jnp.float32) * 0.1, 'edge_Wih': jax.random.normal(ks[5], (3 * H, H), jnp.float32) * std, 'edge_Whh': jax.random.normal(ks[6], (3 * H, H), jnp.float32) * std, 'edge_bih': jnp.zeros((3 * H,), jnp.float32), 'edge_bhh': jnp.zeros((3 * H,), jnp.float32), 'node_Wih': jax.random.normal(ks[7], (3 * H, H), jnp.float32) * std, 'node_Whh': jax.random.normal(ks[8], (3 * H, H), jnp.float32) * std, 'node_bih': jnp.zeros((3 * H,), jnp.float32), 'node_bhh': jnp.zeros((3 * H,), jnp.float32)}
    _L3_gnn_all = _L3_gnn_setup()
    _L3_gnn_in = {k: v for k, v in _L3_gnn_all.items() if k in ('gat_W', 'gat_a', 'edge_Wih', 'edge_Whh', 'edge_bih', 'edge_bhh', 'node_Wih', 'node_Whh', 'node_bih', 'node_bhh')}
    del _L3_gnn_all
    return {'x': x, 'adj': adj, 'L0_gnn_W': _L0_gnn_in['W'], 'L1_gnn_W1': _L1_gnn_in['W1'], 'L1_gnn_b1': _L1_gnn_in['b1'], 'L1_gnn_W2': _L1_gnn_in['W2'], 'L1_gnn_b2': _L1_gnn_in['b2'], 'L1_gnn_W3': _L1_gnn_in['W3'], 'L1_gnn_b3': _L1_gnn_in['b3'], 'L1_gnn_g1': _L1_gnn_in['g1'], 'L1_gnn_be1': _L1_gnn_in['be1'], 'L1_gnn_g2': _L1_gnn_in['g2'], 'L1_gnn_be2': _L1_gnn_in['be2'], 'L1_gnn_g3': _L1_gnn_in['g3'], 'L1_gnn_be3': _L1_gnn_in['be3'], 'L2_gnn_weight': _L2_gnn_in['weight'], 'L2_gnn_bias': _L2_gnn_in['bias'], 'L3_gnn_gat_W': _L3_gnn_in['gat_W'], 'L3_gnn_gat_a': _L3_gnn_in['gat_a'], 'L3_gnn_edge_Wih': _L3_gnn_in['edge_Wih'], 'L3_gnn_edge_Whh': _L3_gnn_in['edge_Whh'], 'L3_gnn_edge_bih': _L3_gnn_in['edge_bih'], 'L3_gnn_edge_bhh': _L3_gnn_in['edge_bhh'], 'L3_gnn_node_Wih': _L3_gnn_in['node_Wih'], 'L3_gnn_node_Whh': _L3_gnn_in['node_Whh'], 'L3_gnn_node_bih': _L3_gnn_in['node_bih'], 'L3_gnn_node_bhh': _L3_gnn_in['node_bhh']}

def reference(x, adj, L0_gnn_W, L1_gnn_W1, L1_gnn_b1, L1_gnn_W2, L1_gnn_b2, L1_gnn_W3, L1_gnn_b3, L1_gnn_g1, L1_gnn_be1, L1_gnn_g2, L1_gnn_be2, L1_gnn_g3, L1_gnn_be3, L2_gnn_weight, L2_gnn_bias, L3_gnn_gat_W, L3_gnn_gat_a, L3_gnn_edge_Wih, L3_gnn_edge_Whh, L3_gnn_edge_bih, L3_gnn_edge_bhh, L3_gnn_node_Wih, L3_gnn_node_Whh, L3_gnn_node_bih, L3_gnn_node_bhh):
    import jax
    import jax.numpy as jnp

    def _L0_gnn_ref(features, adj, W):
        import jax, jax.numpy as jnp
        import numpy as np
        N = 8192
        D = 128
        OUT = 128
        deg = adj.sum(axis=1, keepdims=True) + 1.0
        neigh = adj @ features / deg
        data = jnp.concatenate([features, neigh], axis=-1)
        return data @ W.T

    def _L1_gnn_ref(x, adj, W1, b1, W2, b2, W3, b3, g1, be1, g2, be2, g3, be3):
        import jax, jax.numpy as jnp
        import numpy as np
        N = 4096
        EMB = 128
        EDGE_P = 0.004
        LN_EPS = 1e-05

        def _layernorm(h, g, b):
            mu = jnp.mean(h, axis=-1, keepdims=True)
            var = jnp.mean(jnp.square(h - mu), axis=-1, keepdims=True)
            return (h - mu) * jax.lax.rsqrt(var + LN_EPS) * g + b
        dinv = jnp.sum(adj, axis=-1) ** (-0.5)
        A = adj * dinv[:, None] * dinv[None, :]
        h1 = x @ W1 + b1
        n1 = _layernorm(jax.nn.relu(A @ h1) + h1, g1, be1)
        h2 = n1 @ W2 + b2
        n2 = _layernorm(jax.nn.relu(A @ h2) + n1, g2, be2)
        h3 = n2 @ W3 + b3
        n3 = _layernorm(jax.nn.relu(A @ h3) + n2, g3, be3)
        return n3

    def _L2_gnn_ref(input, adj, weight, bias):
        import jax, jax.numpy as jnp
        import numpy as np
        N = 4096
        F_IN = 128
        F_OUT = 128
        n = input.shape[0]
        a = adj + jnp.eye(n, dtype=adj.dtype)
        d = jax.lax.rsqrt(jnp.sum(a, axis=1))
        adj_norm = d[:, None] * a * d[None, :]
        support = input @ weight
        out = adj_norm @ support + bias
        return out

    def _L3_gnn_ref(h, node_adj, edge_adj, gat_W, gat_a, edge_Wih, edge_Whh, edge_bih, edge_bhh, node_Wih, node_Whh, node_bih, node_bhh):
        import jax, jax.numpy as jnp
        import numpy as np
        N, H, HEADS = (2048, 128, 3)
        ALPHA = 0.2
        NEG_INF = -9000000000000000.0

        def _sign_adj(key, n, density):
            k1, k2 = jax.random.split(key)
            mask = jax.random.uniform(k1, (n, n)) < density
            sign = jnp.where(jax.random.uniform(k2, (n, n)) < 0.5, -1.0, 1.0)
            adj = jnp.where(mask, sign, 0.0).astype(jnp.float32)
            idx = jnp.arange(n)
            return adj.at[idx, idx].set(1.0)

        def _gru_cell(x, hstate, Wih, Whh, bih, bhh):
            gi = x @ Wih.T + bih
            gh = hstate @ Whh.T + bhh
            ir, iz, inn = jnp.split(gi, 3, axis=1)
            hr, hz, hn = jnp.split(gh, 3, axis=1)
            r = jax.nn.sigmoid(ir + hr)
            z = jax.nn.sigmoid(iz + hz)
            n = jnp.tanh(inn + r * hn)
            return (1.0 - z) * n + z * hstate

        def _gat_head(h, node_adj, edge_adj, W, a):
            hW = h @ W
            hp = (node_adj > 0).astype(hW.dtype) @ hW
            hm = (node_adj < 0).astype(hW.dtype) @ hW
            e_plus = jax.nn.leaky_relu(jnp.concatenate([hp, hm], axis=1) @ a, ALPHA)[:, 0]
            e_minus = jax.nn.leaky_relu(jnp.concatenate([hm, hp], axis=1) @ a, ALPHA)[:, 0]
            att = jnp.where(edge_adj > 0, e_plus[None, :], NEG_INF)
            att = jnp.where(edge_adj < 0, e_minus[None, :], att)
            att = jax.nn.softmax(att, axis=1)
            return att * edge_adj @ hW
        dn = jnp.diag(node_adj)
        de = jnp.diag(edge_adj)
        idx = jnp.arange(node_adj.shape[0])
        node_adj_norm = node_adj.at[idx, idx].add(-dn)
        edge_adj_norm = edge_adj.at[idx, idx].add(-de)
        node_support = node_adj_norm @ h
        edge_output = _gru_cell(node_support, h, edge_Wih, edge_Whh, edge_bih, edge_bhh)
        edge_support = _gat_head(h, node_adj_norm, edge_adj_norm, gat_W[0], gat_a[0])
        for i in range(1, HEADS):
            edge_support = edge_support + _gat_head(h, node_adj_norm, edge_adj_norm, gat_W[i], gat_a[i])
        edge_support = edge_support / HEADS
        node_output = _gru_cell(edge_support, h, node_Wih, node_Whh, node_bih, node_bhh)
        return de[:, None] * edge_output + dn[:, None] * node_output
    x = _layernorm(x + _L0_gnn_ref(x, adj, L0_gnn_W), axis=-1)
    x = _layernorm(x + _L1_gnn_ref(x, adj, L1_gnn_W1, L1_gnn_b1, L1_gnn_W2, L1_gnn_b2, L1_gnn_W3, L1_gnn_b3, L1_gnn_g1, L1_gnn_be1, L1_gnn_g2, L1_gnn_be2, L1_gnn_g3, L1_gnn_be3), axis=-1)
    x = _layernorm(x + _L2_gnn_ref(x, adj, L2_gnn_weight, L2_gnn_bias), axis=-1)
    x = _layernorm(x + _L3_gnn_ref(x, adj, adj, L3_gnn_gat_W, L3_gnn_gat_a, L3_gnn_edge_Wih, L3_gnn_edge_Whh, L3_gnn_edge_bih, L3_gnn_edge_bhh, L3_gnn_node_Wih, L3_gnn_node_Whh, L3_gnn_node_bih, L3_gnn_node_bhh), axis=-1)
    return x

_drawn_inputs = setup_inputs


def setup_inputs(seed=0):
    import zlib

    import numpy as np

    out = dict(_drawn_inputs(seed))
    spreads = {'L1_gnn_g1': (1.0, 0.2),
     'L1_gnn_be1': (0.0, 0.1),
     'L1_gnn_g2': (1.0, 0.2),
     'L1_gnn_be2': (0.0, 0.1),
     'L1_gnn_g3': (1.0, 0.2),
     'L1_gnn_be3': (0.0, 0.1),
     'L3_gnn_edge_bih': (0.0, 0.482),
     'L3_gnn_edge_bhh': (0.0, 0.694),
     'L3_gnn_node_bih': (0.0, 0.435),
     'L3_gnn_node_bhh': (0.0, 0.632)}
    factors = {'L3_gnn_gat_W': 5.968,
     'L3_gnn_gat_a': 7.245,
     'L3_gnn_edge_Whh': 4.303,
     'L3_gnn_node_Wih': 5.831,
     'L3_gnn_node_Whh': 4.208}
    for name, (base, spread) in spreads.items():
        noise = np.random.default_rng([zlib.crc32(name.encode()), seed]).standard_normal(out[name].shape)
        drawn = base * np.exp(spread * noise) if base else spread * noise
        out[name] = jnp.asarray(drawn.astype(out[name].dtype))
    for name, factor in factors.items():
        out[name] = (out[name] * factor).astype(out[name].dtype)
    return out
```

```python
from contextlib import ExitStack

import concourse.bass as bass
from concourse import mybir

ALU = mybir.AluOpType
ACT = mybir.ActivationFunctionType
F32 = mybir.dt.float32
BF16 = mybir.dt.bfloat16
I16 = mybir.dt.int16
AXX = mybir.AxisListType.X

N = 3327
P = 128
D = 128
T = -(-N // P)
W = 256
B = T * P // W
IT = W // P
HALF = T // 2
HEADS = 3
V = 2 * HEADS
EPS = 1e-5
ALPHA = 0.2
LOG2E = 1.4426950408889634
LN2_HI = 0.693359375
LN2_LO = -2.12194440e-4
ROUND = 12582912.0
NMAX = float(2 ** 20 - 2)
SHIFT = float(2 ** 20)
TINY = 1e-30

C_WAB, C_W1, C_W4, C_GW, C_GWT, C_GA = 0, 256, 640, 768, 1152, 1536
C_GB = C_GA + 6
C_END = C_GB + 7 * D
R_B, R_BIH, R_BHH, R_END = 0, 384, 768, 1152

class Block:

    def __init__(self, c, r=0):
        self.c, self.r = c, r

    def at(self, k, base=0):
        return self.r * (2 * k) + (base + k * self.c)

    def cols(self, k):
        return bass.ds(self.at(k), k)


def sweep(eng, step):
    step(Block(0), None)
    with eng.Fori(0, (B - 1) // 2) as r:
        step(Block(1, r), Block(0, r))
        step(Block(2, r), Block(1, r))
    step(None, Block(B - 1))


def build(nc, adjt, diag, xrow, xcol, consts, rows, gru, gru_rows, ident, out):
    ctx = ExitStack()
    with ctx:
        def sb(name, shape, dt=F32):
            return ctx.enter_context(nc.sbuf_tensor(name, shape, dt))

        def sem(name):
            return ctx.enter_context(nc.semaphore(name))

        ring = sb("ring", [P, 2, T, W])
        X = sb("X", [P, T, D])
        res_eo = sb("res_eo", [P, T, D])
        xt_es = sb("xt_es", [P, T * D])
        FW = sb("FW", [P, 2, T * D])
        HW = sb("HW", [P, T, HEADS * D])
        region_m = sb("region_m", [P, T * W])
        region_t = sb("region_t", [P, T * D])
        stage = sb("stage", [P, 2048])
        idn = sb("idn", [P, P])
        ones = sb("ones", [P, P])
        dg = sb("dg", [P, T])
        norm = sb("norm", [P, T, 2])
        small = sb("small", [P, 48])
        e_f = sb("e_f", [P, T, V])
        nbits = sb("nbits", [P, T, V])
        nneg = sb("nneg", [P, T, V])
        fpart = sb("fpart", [P, T, V, 3], BF16)

        cst = region_m[:, 0:C_END]
        wab = cst[:, C_WAB:C_WAB + 2 * D]
        gat_w = cst[:, C_GW:C_GW + HEADS * D]
        gat_wt = cst[:, C_GWT:C_GWT + HEADS * D]
        gat_a = cst[:, C_GA:C_GA + V]
        wa = region_m[:, C_END:C_END + V]

        def gb(k):
            return cst[:, C_GB + k * D:C_GB + (k + 1) * D]

        brow = region_t[0:1, 0:R_END]
        wih = region_t[:, R_END:R_END + 3 * D]
        whh = region_t[:, R_END + 3 * D:R_END + 6 * D]
        o = R_END + 6 * D
        xts = region_t[:, o:o + W]
        colsum = region_t[:, o + W:o + 3 * W].rearrange("p (h c) -> p h c", h=2)
        o += 3 * W
        uraw = region_t[:, o:o + T * V].rearrange("p (t v) -> p t v", v=V)
        o += T * V
        upos = region_t[:, o:o + T * 9].bitcast(BF16).rearrange("p (t k) -> p t k", k=3 * V)
        o += T * 9
        uneg = region_t[:, o:o + T * 9].bitcast(BF16).rearrange("p (t k) -> p t k", k=3 * V)
        assert o + T * 9 <= T * D

        mask5 = region_m[:, :].bitcast(BF16).rearrange("p (h s t c) -> p h s t c", h=2, s=2, t=HALF)
        mask6 = region_m[:, :].bitcast(I16).rearrange("p (s t c) -> p s t c", s=2, t=T)
        pow_i = region_t[:, :].bitcast(I16).rearrange("p (k t c) -> p k t c", k=2, t=HALF)
        pow_b = region_t[:, :].bitcast(BF16).rearrange("p (k t c) -> p k t c", k=2, t=HALF)
        weight = FW[:, :, :].rearrange("p k (t c) -> p k t c", t=HALF)
        heads_t = region_t[:, 0:HEADS * W].rearrange("p (h c) -> p h c", h=HEADS)

        def stg(k):
            return stage[:, k * W:(k + 1) * W]
        xs, zs, xTs, ys, gn, gt = (stg(k) for k in (0, 1, 2, 3, 6, 7))
        gates = stage[:, 4 * W:6 * W].rearrange("p (i c) -> p i c", i=IT)
        kmax = stage[:, 0:3 * W].rearrange("p (h c) -> p h c", h=HEADS)
        negk = stage[:, 3 * W:6 * W].rearrange("p (h c) -> p h c", h=HEADS)

        def two(ap):
            return ap.rearrange("p (i f) -> p i f", i=IT)

        sd = small[:, 0:4].rearrange("p (i k) -> p i k", i=IT)
        rec = small[:, 4:6]
        drec = small[:, 6:8]
        bs = small[:, 8:20].rearrange("p (i k) -> p i k", i=IT)
        mv = small[:, 20:24].rearrange("p (i k) -> p i k", i=IT)
        std = small[:, 24:28]
        rstd = small[:, 28:30]
        eps = small[:, 30:31]
        diag1 = small[:, 31:33]
        zz = small[:, 33:39].rearrange("p (i h) -> p i h", i=IT)
        rz = small[:, 39:45].rearrange("p (i h) -> p i h", i=IT)

        def ps(name, banks=1):
            return ctx.enter_context(nc.psum_tensor(name, [P, 512 * banks], F32))
        Z = [ps("Z0"), ps("Z1")]
        TP, HB, HC, ST = ps("TP"), ps("HB"), ps("HC"), ps("ST")
        E = ps("E", 2).rearrange("p (i c) -> p i c", i=IT)
        NUM = [Z[0][:, 0:W], Z[1][:, 0:W], TP[:, 0:W]]
        tp, hb, hc = (x[:, 0:W] for x in (TP, HB, HC))
        hsum = [hb, HB[:, W:2 * W], hc]

        s_c = sem("constants_in")
        s_x = sem("x_in")
        s_g = sem("edge_weights_in")
        s_n = sem("node_weights_in")
        arrived = [[sem(f"arrived_{s}{h}") for h in range(2)] for s in range(2)]
        s_init = sem("init_done")
        s_pe = sem("pe_half_done")
        s_dve = sem("dve_half_done")
        s_wa = sem("wa_product")
        s_was = sem("wa_stored")
        s_zs = sem("zs_ready")
        s_a = sem("closing_a_done")
        s_var = sem("to_sqrt")
        s_std = sem("sqrt_done")
        s_d1 = sem("rows_ready")
        s_b = sem("rows_transposed")
        s_xt = sem("xTs_ready")
        s_cc = sem("closing_c_done")
        s_d2 = sem("operand_ready")
        s_u = sem("u_parts_ready")
        s_m5 = sem("sign_masks_ready")
        s_s5 = sem("logits_half_done")
        s_e5 = sem("logits_read")
        s_sig = sem("sigmoid_done")
        s_th = sem("to_tanh")
        s_tn = sem("tanh_done")
        s_go = sem("gru_done")
        s_ex = sem("to_exp")
        s_f = sem("exp_done")
        s_fp = sem("f_parts_ready")
        s_mx = sem("max_ready")
        s_par = sem("max_reduced")
        s_nk = sem("negk_ready")
        s_t = sem("powers_ready")
        s_tm = sem("powers_masked")
        s_w = sem("weights_ready")
        s_c6 = sem("chunk_done")
        s_ev = sem("heads_copied")
        s_tr = sem("heads_transposed")
        s_es = sem("heads_summed")
        s_q = sem("dve_chain")
        s_qa = sem("act_chain")
        s_out = sem("out_written")
        s_fin = sem("final_rows")

        VAR = [2, 1, 1, 2, 1]
        vbase = [B * sum(VAR[:p]) for p in range(6)]

        def wait(eng, semaphore, value):
            if not (isinstance(value, int) and value <= 0):
                eng.wait_ge(semaphore, value)

        def alone(eng):
            eng.nop(nofuse=True)

        class Links:

            def __init__(self, eng, semaphore):
                self.eng, self.sem = eng, semaphore
                self.done, self.turn = 0, 0

            def link(self, ins):
                ins.then_inc(self.sem, 1)
                self.done += 1
                self.eng.wait_ge(self.sem, self.turn + self.done)

            def sweep(self, step, per):
                step(Block(0), None)
                before = self.done
                with self.eng.Fori(0, (B - 1) // 2) as r:
                    self.turn = r * per
                    step(Block(1, r), Block(0, r))
                    step(Block(2, r), Block(1, r))
                self.turn = 0
                assert self.done - before == per, (self.done - before, per)
                self.done = before + per * ((B - 1) // 2)
                step(None, Block(B - 1))

        def slot(p, blk):
            return (p * B + blk.c) % 2

        def uses(p, blk, k=0):
            return blk.r * 16 + 16 * ((p * B + blk.c) // 2 + 1)

        def g(p, blk, k, more=0):
            return blk.at(k, k * p * B + more)

        block = ctx.enter_context(nc.Block())

        @block.sync
        def _(sp):
            sp.dma_start(cst, consts).then_inc(s_c, 16)
            sp.dma_start(FW[:, 0, :], xrow).then_inc(s_x, 16)
            sp.dma_start(xt_es[:, :], xcol).then_inc(s_x, 16)
            sp.dma_start(dg[:, :], diag).then_inc(s_c, 16)
            sp.dma_start(idn[:, :], ident).then_inc(s_c, 16)
            sp.dma_start(brow, rows).then_inc(s_c, 16)
            sp.dma_start(region_t[:, R_END:R_END + 6 * D], gru[0]).then_inc(s_g, 16)

            def load(p, blk, pe_wait=None, dve_wait=None):
                for h in range(2):
                    if pe_wait is not None:
                        sp.wait_ge(s_pe, pe_wait(h))
                    if dve_wait is not None:
                        alone(sp)
                        sp.wait_ge(s_dve, dve_wait(h))
                    src = adjt[bass.ds(blk.at(1), 1), :, h * HALF:(h + 1) * HALF, :]
                    sp.dma_start(ring[:, slot(p, blk), h * HALF:(h + 1) * HALF, :],
                                 src.rearrange("a p t c -> (a p) t c"))\
                        .then_inc(arrived[slot(p, blk)][h], 16)

            DB = {0: 0, 5: 2 * B, 6: 4 * B}
            for p in range(7):
                def pe_wait(blk):
                    if p == 6:
                        return None
                    return lambda h: g(p, blk, 2, h - 3)

                def dve_wait(blk):
                    if p not in DB:
                        return None
                    return lambda h: blk.at(2, DB[p] + h - 3)

                for c in range(2):
                    if p == 0:
                        load(p, Block(c))
                    elif p == 6:
                        load(p, Block(c), lambda h: 2 * 6 * B, dve_wait(Block(c)))
                    elif p == 5:
                        load(p, Block(c), pe_wait(Block(c)))
                    else:
                        load(p, Block(c), pe_wait(Block(c)), (lambda h: 2 * B) if p == 1 else None)
                with sp.Fori(0, (B - 3) // 2) as r:
                    load(p, Block(2, r), pe_wait(Block(2, r)), dve_wait(Block(2, r)))
                    load(p, Block(3, r), pe_wait(Block(3, r)), dve_wait(Block(3, r)))
                last = Block(B - 1)
                load(p, last, pe_wait(last), dve_wait(last))
            sp.wait_ge(s_tr, B)
            sp.wait_ge(s_c6, 12 * B)
            sp.dma_start(region_t[0:1, 0:6 * D], gru_rows).then_inc(s_n, 16)
            sp.dma_start(region_t[:, R_END:R_END + 6 * D], gru[1]).then_inc(s_n, 16)
            sp.wait_ge(s_fin, 1)
            sp.dma_start(out.rearrange("(t p) f -> p t f", p=P), res_eo[:, :, :]).then_inc(s_out, 16)
            sp.wait_ge(s_out, 16)

        @block.tensor
        def _(pe):
            pe.wait_ge(s_c, 64)
            pe.wait_ge(s_g, 16)
            pe.wait_ge(s_init, 4)
            for h in range(HEADS):
                last = pe.matmul(ST[:, 2 * h:2 * h + 2], gat_wt[:, h * D:(h + 1) * D],
                                 gat_a[:, 2 * h:2 * h + 2], start=True, stop=True)
            last.then_inc(s_wa, 1)
            pe.wait_ge(s_x, 32)

            def main(p, blk, t0, t1):
                zz_ = Z[slot(p, blk)][:, 0:W]
                for t in range(t0, t1):
                    if t in (0, HALF):
                        pe.wait_ge(arrived[slot(p, blk)][t // HALF], uses(p, blk))
                    f = X[:, t, :] if p == 5 else FW[:, p % 2, t * D:(t + 1) * D]
                    mm = pe.matmul(zz_, f, ring[:, slot(p, blk), t, :], start=t == 0, stop=t == T - 1)
                    if t in (HALF - 1, T - 1):
                        mm.then_inc(s_pe, 1)

            def step_a(p, blk):
                pe.wait_ge(s_zs, g(p, blk, 1, 1))
                if p == 0:
                    pe.wait_ge(s_dve, blk.at(2, 2))
                    for i in range(IT):
                        s = slice(i * P, (i + 1) * P)
                        pe.matmul(E[:, i, 0:2 * D], xts[:, s], wab, start=True, stop=True)
                        pe.matmul(E[:, i, 2 * D:3 * D], zs[:, s], wab[:, D:2 * D], start=True, stop=True)
                        pe.matmul(E[:, i, 3 * D:3 * D + 1], colsum[:, 0, s], ones[:, 0:1], start=True, stop=False)
                        last = pe.matmul(E[:, i, 3 * D:3 * D + 1], colsum[:, 1, s], ones[:, 0:1],
                                         start=False, stop=True)
                    last.then_inc(s_a, 1)
                else:
                    for i in range(IT):
                        last = pe.transpose(two(tp)[:, i, :], zs[:, i * P:(i + 1) * P], idn[:, :])
                    last.then_inc(s_a, 1)

            def step_b(p, blk):
                pe.wait_ge(s_d1, g(p, blk, 1, 1))
                for i in range(IT):
                    last = pe.transpose(two(hb)[:, i, :], xs[:, i * P:(i + 1) * P], idn[:, :])
                last.then_inc(s_b, 1)

            def step_c(p, blk):
                if p == 3:
                    wgt = cst[:, C_W4:C_W4 + D]
                elif p < 3:
                    wgt = cst[:, C_W1 + p * D:C_W1 + (p + 1) * D]
                pe.wait_ge(s_xt, g(p, blk, 1, 1))
                for i in range(IT):
                    lhs = xTs[:, i * P:(i + 1) * P]
                    if p == 4:
                        pe.matmul(E[:, i, 0:3 * D], lhs, gat_w, start=True, stop=True)
                        last = pe.matmul(E[:, i, 3 * D:3 * D + V], lhs, wa, start=True, stop=True)
                    else:
                        last = pe.matmul(two(hc)[:, i, :], lhs, wgt, start=i == 0, stop=p == 3,
                                         skip_group_check=True)
                        if p < 3:
                            last = pe.matmul(two(hc)[:, i, :], ones[0:1, :],
                                             brow[:, R_B + p * D:R_B + (p + 1) * D],
                                             start=False, stop=True, skip_group_check=True)
                last.then_inc(s_cc, 1)

            for p in range(5):
                if p > 0:
                    pe.wait_ge(s_d2, p * B)
                if p == 0:
                    pe.wait_ge(s_was, 1)

                def step(mb, eb):
                    if mb:
                        main(p, mb, 0, 9)
                    if eb:
                        step_a(p, eb)
                    if mb:
                        main(p, mb, 9, 18)
                    if eb:
                        step_b(p, eb)
                    if mb:
                        main(p, mb, 18, T)
                    if eb:
                        step_c(p, eb)
                sweep(pe, step)

            def gru_products(bias):
                for i in range(IT):
                    s = slice(i * P, (i + 1) * P)
                    pe.matmul(E[:, i, 0:3 * D], zs[:, s], wih, start=True, stop=False, skip_group_check=True)
                    pe.matmul(E[:, i, 0:2 * D], xTs[:, s], whh[:, 0:2 * D], start=False, stop=False,
                              skip_group_check=True)
                    pe.matmul(E[:, i, 3 * D:4 * D], xTs[:, s], whh[:, 2 * D:3 * D], start=False, stop=False,
                              skip_group_check=True)
                    pe.matmul(E[:, i, 0:3 * D], ones[0:1, :], bias[:, 0:3 * D], start=False, stop=False,
                              skip_group_check=True)
                    pe.matmul(E[:, i, 0:2 * D], ones[0:1, :], bias[:, 3 * D:5 * D], start=False, stop=True,
                              skip_group_check=True)
                    last = pe.matmul(E[:, i, 3 * D:4 * D], ones[0:1, :], bias[:, 5 * D:6 * D],
                                     start=False, stop=True, skip_group_check=True)
                last.then_inc(s_cc, 1)

            def logits(blk, h):
                pe.wait_ge(s_m5, blk.at(2, h + 1))
                if h == 0:
                    wait(pe, s_e5, blk.at(1))
                for t in range(HALF):
                    for i in range(IT):
                        for s, u in ((0, upos), (1, uneg)):
                            first = h == 0 and t == 0 and i == 0 and s == 0
                            last = pe.matmul(ST[:, i * 3 * V:(i + 1) * 3 * V],
                                             mask5[:, h, s, t, i * P:(i + 1) * P], u[:, h * HALF + t, :],
                                             start=first, stop=h == 1 and t == HALF - 1 and s == 1,
                                             skip_group_check=True)
                last.then_inc(s_s5, 1)

            pe.wait_ge(s_d2, 5 * B)
            pe.wait_ge(s_u, 1)

            def step5(mb, eb):
                if mb:
                    main(5, mb, 0, HALF)
                if eb:
                    step_b(5, eb)
                if mb:
                    logits(mb, 0)
                    main(5, mb, HALF, T)
                if eb:
                    pe.wait_ge(s_zs, g(5, eb, 1, 1))
                    pe.wait_ge(s_xt, g(5, eb, 1, 1))
                    gru_products(brow[:, R_BIH:R_END])
                if mb:
                    logits(mb, 1)
            sweep(pe, step5)

            pe.wait_ge(s_fp, 1)
            pe.wait_ge(s_zs, 6 * B)

            def chunks(blk):
                wait(pe, s_es, blk.at(1))
                wait(pe, s_ev, blk.at(1))
                for c in range(2 * V):
                    v, half = divmod(c, 2)
                    h = v % HEADS
                    pe.wait_ge(s_tm, blk.at(2 * V, c + 1))
                    for t in range(HALF):
                        for i in range(IT):
                            k = i * 9 + h * 3
                            pe.matmul(ST[:, k:k + 3], pow_b[:, c % 2, t, i * P:(i + 1) * P],
                                      fpart[:, half * HALF + t, v, :],
                                      start=c == 0 and t == 0 and i == 0,
                                      stop=v >= HEADS and half == 1 and t == HALF - 1,
                                      skip_group_check=True)
                    pe.wait_ge(s_w, blk.at(2 * V, c + 1))
                    for t in range(HALF):
                        last = pe.matmul(NUM[h], HW[:, half * HALF + t, h * D:(h + 1) * D],
                                         weight[:, c % 2, t, :], start=v < HEADS and half == 0 and t == 0,
                                         stop=v >= HEADS and half == 1 and t == HALF - 1)
                    last.then_inc(s_c6, 1)
                pe.wait_ge(s_ev, blk.at(1, 1))
                for h in range(HEADS):
                    for i in range(IT):
                        last = pe.transpose(two(hsum[h])[:, i, :], heads_t[:, h, i * P:(i + 1) * P], idn[:, :])
                last.then_inc(s_tr, 1)
            chunks(Block(0))
            with pe.Fori(0, (B - 1) // 2) as r:
                chunks(Block(1, r))
                chunks(Block(2, r))

            pe.wait_ge(s_n, 32)

            def step7(blk):
                pe.wait_ge(s_d1, g(6, blk, 1, 1))
                for i in range(IT):
                    pe.transpose(two(hb)[:, i, :], xs[:, i * P:(i + 1) * P], idn[:, :])
                for i in range(IT):
                    last = pe.transpose(two(tp)[:, i, :], ys[:, i * P:(i + 1) * P], idn[:, :])
                last.then_inc(s_b, 1)
                pe.wait_ge(s_xt, g(6, blk, 1, 1))
                pe.wait_ge(s_go, g(1, blk, 1, 1))
                gru_products(region_t[0:1, 0:6 * D])
            step7(Block(0))
            with pe.Fori(0, (B - 1) // 2) as r:
                step7(Block(1, r))
                step7(Block(2, r))

        @block.scalar
        def _(act):
            act.wait_ge(s_x, 32)
            act.wait_ge(s_init, 4)
            act.wait_ge(s_wa, 1)
            act.activation(wa.rearrange("p (k h) -> p h k", k=2),
                           ST[:, 0:V].rearrange("p (h k) -> p h k", k=2), ACT.Copy).then_inc(s_was, 1)

            def copy_z(p, blk):
                act.wait_ge(s_pe, g(p, blk, 2, 2))
                if p == 0:
                    act.activation(xts, xt_es[:, blk.cols(W)], ACT.Copy)
                act.activation(zs, Z[slot(p, blk)][:, 0:W], ACT.Copy).then_inc(s_zs, 1)

            def copy_xt(p, blk):
                act.wait_ge(s_b, g(p, blk, 1, 1))
                act.activation(xTs, hb, ACT.Copy).then_inc(s_xt, 1)

            for p in range(5):
                def step(mb, eb):
                    if not eb:
                        return
                    copy_z(p, eb)
                    if p == 0:
                        act.wait_ge(s_var, eb.at(2, 1))
                        act.activation(std[:, 0:4], small[:, 0:4], ACT.Sqrt).then_inc(s_std, 1)
                    for k in range(1 if p == 0 else 0, VAR[p]):
                        act.wait_ge(s_var, eb.at(VAR[p], vbase[p] + k + 1))
                        act.activation(std[:, 0:2], mv[:, :, 1], ACT.Sqrt, bias=eps).then_inc(s_std, 1)
                    copy_xt(p, eb)
                sweep(act, step)

            def gate_functions(n):
                act.wait_ge(s_cc, n(1 + 5 * B))
                alone(act)
                act.wait_ge(s_go, n(1))
                act.activation(gates[:, :, :], E[:, :, 0:2 * D], ACT.Sigmoid).then_inc(s_sig, 1)
                act.wait_ge(s_th, n(1))
                act.activation(gn, gt, ACT.Tanh).then_inc(s_tn, 1)

            def step5(mb, eb):
                if not eb:
                    return
                act.wait_ge(s_cc, g(5, eb, 1))
                act.activation(xs, X[:, eb.cols(IT), :].rearrange("p i f -> p (i f)"), ACT.Copy)\
                    .then_inc(s_d1, 1)
                copy_z(5, eb)
                copy_xt(5, eb)
                gate_functions(lambda k: eb.at(1, k))
            sweep(act, step5)

            act.wait_ge(s_ex, 1)
            act.activation(e_f[:, :, :], nbits[:, :, :], ACT.Exp).then_inc(s_f, 1)

            def powers(blk):
                for c in range(2 * V):
                    v, half = divmod(c, 2)
                    if c == 0:
                        act.wait_ge(s_fp, 1)
                        wait(act, s_tr, blk.at(1))
                        act.wait_ge(s_nk, blk.at(1, 1))
                    wait(act, s_c6, blk.at(2 * V, c - 1))
                    for t in range(HALF):
                        tt = half * HALF + t
                        last = act.activation(pow_i[:, c % 2, t, :], negk[:, v % HEADS, :], ACT.Relu,
                                              bias=nbits[:, tt, v:v + 1])
                    last.then_inc(s_t, 1)
                act.wait_ge(s_c6, blk.at(2 * V, 2 * V))
                for h in range(HEADS):
                    last = act.activation(heads_t[:, h, :], NUM[h], ACT.Copy)
                last.then_inc(s_ev, 1)
            powers(Block(0))
            with act.Fori(0, (B - 1) // 2) as r:
                powers(Block(1, r))
                powers(Block(2, r))

            act.wait_ge(s_es, B)

            def step7(blk):
                act.wait_ge(s_cc, g(6, blk, 1))
                act.activation(xs, X[:, blk.cols(IT), :].rearrange("p i f -> p (i f)"), ACT.Copy)
                act.activation(ys, xt_es[:, blk.cols(W)], ACT.Copy).then_inc(s_d1, 1)
                act.wait_ge(s_b, g(6, blk, 1, 1))
                act.activation(zs, tp, ACT.Copy)
                act.activation(xTs, hb, ACT.Copy).then_inc(s_xt, 1)
                gate_functions(lambda k: blk.at(1, B + k))
            step7(Block(0))
            with act.Fori(0, (B - 1) // 2) as r:
                step7(Block(1, r))
                step7(Block(2, r))
            act.wait_ge(s_var, vbase[5] + 1)
            act.activation(norm[:, :, 0], norm[:, :, 1], ACT.Sqrt, bias=eps).then_inc(s_std, 1)

        @block.gpsimd
        def _(pool):
            def reduce(blk):
                for h in range(HEADS):
                    pool.wait_ge(s_mx, blk.at(HEADS, h + 1))
                    if h == 0:
                        wait(pool, s_t, blk.at(2 * V))
                    alone(pool)
                    pool.partition_all_reduce(negk[:, h, :], kmax[:, h, :], P, bass.bass_isa.ReduceOp.max)\
                        .then_inc(s_par, 1)
            reduce(Block(0))
            with pool.Fori(0, (B - 1) // 2) as r:
                reduce(Block(1, r))
                reduce(Block(2, r))

        @block.vector
        def _(dve):
            q = Links(dve, s_q)
            link = q.link
            dve.memset(ones[:, :], 1.0).then_inc(s_init, 1)
            dve.memset(eps, EPS).then_inc(s_init, 1)
            dve.memset(rec, 0.0).then_inc(s_go, 1)
            dve.memset(small[:, 31:48], 0.0).then_inc(s_init, 1)
            dve.memset(colsum, 0.0).then_inc(s_init, 1)
            dve.wait_ge(s_c, 64)
            dve.wait_ge(s_x, 32)
            dve.wait_ge(s_was, 1)

            def layer_norm(y, dst, vwait):
                for i in range(IT):
                    st = dve.bn_stats(bs[:, i, :], two(y)[:, i, :])
                link(st)
                alone(dve)
                for i in range(IT):
                    st = dve.bn_aggr(mv[:, i, :], bs[:, i, :])
                st.then_inc(s_var, 1)
                dve.wait_ge(s_std, vwait)
                link(dve.reciprocal(rstd, std[:, 0:2]))
                for i in range(IT):
                    st = dve.tensor_scalar(two(dst)[:, i, :], two(y)[:, i, :], mv[:, i, 0:1], rstd[:, i:i + 1],
                                           ALU.subtract, ALU.mult)
                link(st)

            def per_row(k):
                return gb(k).rearrange("p (i f) -> p i f", i=1).broadcast_to([P, IT, D])

            def rows(buf, blk):
                return buf[:, blk.cols(IT), :]

            def f_rows(p, blk):
                return FW[:, p % 2, :].rearrange("p (t f) -> p t f", t=T)[:, blk.cols(IT), :]

            def col(ap, blk, i):
                return ap[:, bass.ds(blk.at(IT, i), 1)]

            def sums(blk):
                for h in range(2):
                    dve.wait_ge(arrived[slot(0, blk)][h], uses(0, blk))
                    if h == 0:
                        wait(dve, s_a, blk.at(1))
                    dve.tensor_reduce(colsum[:, h, :],
                                      ring[:, slot(0, blk), h * HALF:(h + 1) * HALF, :]
                                      .rearrange("p t c -> p c t"), AXX, ALU.add).then_inc(s_dve, 1)

            def close0(blk):
                dve.wait_ge(s_a, blk.at(1, 1))
                link(dve.tensor_tensor(sd[:, :, 0:1], E[:, :, 3 * D:3 * D + 1],
                                       dg[:, blk.cols(IT)].rearrange("p (i k) -> p i k", k=1), ALU.add))
                link(dve.tensor_scalar(sd[:, :, 1], sd[:, :, 0], 1.0, None, ALU.add))
                dve.reciprocal(rec, sd[:, :, 1]).then_inc(s_var, 1)
                dve.wait_ge(s_var, blk.at(2, 1))
                link(dve.tensor_tensor(drec, rec, dg[:, blk.cols(IT)], ALU.mult))
                for i in range(IT):
                    st = dve.tensor_scalar(two(ys)[:, i, :], E[:, i, 2 * D:3 * D], rec[:, i:i + 1], None, ALU.mult)
                link(st)
                for i in range(IT):
                    st = dve.scalar_tensor_tensor(out=two(ys)[:, i, :], in0=E[:, i, D:2 * D],
                                                  scalar=drec[:, i:i + 1], in1=two(ys)[:, i, :],
                                                  op0=ALU.mult, op1=ALU.add)
                link(st)
                link(dve.tensor_tensor(two(ys), E[:, :, 0:D], two(ys), ALU.add))
                link(dve.tensor_tensor(two(ys), f_rows(0, blk), two(ys), ALU.add))
                dve.wait_ge(s_std, blk.at(2, 1))
                link(dve.reciprocal(rows(norm, blk).rearrange("p i k -> p (i k)"), std[:, 0:4]))
                layer_norm(ys, xs, blk.at(2, 2))
                alone(dve)
                dve.tensor_copy(rows(X, blk), two(xs)).then_inc(s_d1, 1)

            def close_l(p, blk):
                dve.wait_ge(s_a, g(p, blk, 1, 1))
                for i in range(IT):
                    st = dve.scalar_tensor_tensor(out=two(ys)[:, i, :],
                                                  in0=FW[:, p % 2, bass.ds(blk.at(W, i * D), D)],
                                                  scalar=col(dg, blk, i), in1=two(tp)[:, i, :],
                                                  op0=ALU.mult, op1=ALU.add)
                link(st)
                for i in range(IT):
                    st = dve.tensor_scalar(two(ys)[:, i, :], two(ys)[:, i, :], norm[:, bass.ds(blk.at(IT, i), 1), 0],
                                           0.0, ALU.mult, ALU.max)
                link(st)
                link(dve.tensor_tensor(two(ys), two(ys), rows(res_eo, blk), ALU.add))
                layer_norm(ys, xs, blk.at(VAR[p], vbase[p] + 1))
                link(dve.tensor_tensor(two(xs), two(xs), per_row(2 * p - 2), ALU.mult))
                if p < 3:
                    link(dve.tensor_tensor(two(xs), two(xs), per_row(2 * p - 1), ALU.add))
                    alone(dve)
                    dve.tensor_copy(rows(res_eo, blk), two(xs)).then_inc(s_d1, 1)
                else:
                    link(dve.tensor_tensor(two(xs), two(xs), per_row(2 * p - 1), ALU.add))
                    link(dve.tensor_tensor(two(ys), two(xs), rows(X, blk), ALU.add))
                    layer_norm(ys, xs, blk.at(VAR[p], vbase[p] + 2))
                    alone(dve)
                    dve.tensor_copy(rows(X, blk), two(xs)).then_inc(s_d1, 1)

            def close4(blk):
                dve.wait_ge(s_a, g(4, blk, 1, 1))
                link(dve.tensor_scalar(diag1, dg[:, blk.cols(IT)], 1.0, None, ALU.add))
                for i in range(IT):
                    st = dve.scalar_tensor_tensor(out=two(ys)[:, i, :],
                                                  in0=FW[:, 0, bass.ds(blk.at(W, i * D), D)],
                                                  scalar=diag1[:, i:i + 1], in1=two(tp)[:, i, :],
                                                  op0=ALU.mult, op1=ALU.add)
                link(st)
                for i in range(IT):
                    st = dve.scalar_tensor_tensor(out=two(ys)[:, i, :], in0=two(ys)[:, i, :],
                                                  scalar=norm[:, bass.ds(blk.at(IT, i), 1), 1], in1=gb(6),
                                                  op0=ALU.mult, op1=ALU.add)
                link(st)
                link(dve.tensor_tensor(two(ys), two(ys), rows(X, blk), ALU.add))
                layer_norm(ys, xs, blk.at(1, vbase[4] + 1))
                alone(dve)
                dve.tensor_copy(rows(X, blk), two(xs)).then_inc(s_d1, 1)

            def operand(p, blk):
                dve.wait_ge(s_cc, g(p, blk, 1, 1))
                if p == 4:
                    alone(dve)
                    dve.tensor_copy(rows(HW, blk), E[:, :, 0:3 * D])
                    alone(dve)
                    dve.tensor_copy(rows(uraw, blk), E[:, :, 3 * D:3 * D + V]).then_inc(s_d2, 1)
                    return
                if p == 0:
                    alone(dve)
                    dve.tensor_copy(rows(res_eo, blk), two(hc))
                for i in range(IT):
                    st = dve.tensor_scalar(FW[:, (p + 1) % 2, bass.ds(blk.at(W, i * D), D)], two(hc)[:, i, :],
                                           norm[:, bass.ds(blk.at(IT, i), 1), 1 if p == 3 else 0], None, ALU.mult)
                st.then_inc(s_d2, 1)

            close = [close0, lambda b: close_l(1, b), lambda b: close_l(2, b), lambda b: close_l(3, b), close4]
            LINKS = [2 * 11, 2 * 8, 2 * 8, 2 * 12, 2 * 7]
            for p in range(5):
                def step(mb, eb):
                    if mb and p == 0:
                        sums(mb)
                    if eb:
                        close[p](eb)
                        operand(p, eb)
                q.sweep(step, LINKS[p])

            dve.wait_ge(s_d2, 5 * B)
            tmp = region_m[:, 0:T * V].rearrange("p (t v) -> p t v", v=V)

            def three_parts(src, parts):
                for k in range(3):
                    link(dve.tensor_copy(parts(k), src))
                    if k < 2:
                        link(dve.tensor_tensor(src, src, parts(k), ALU.subtract))
            dve.wait_ge(s_cc, 5 * B)
            three_parts(uraw, lambda k: upos[:, :, k * V:(k + 1) * V])
            for k in range(3):
                for a in range(2):
                    st = dve.tensor_copy(uneg[:, :, k * V + a * HEADS:k * V + (a + 1) * HEADS],
                                         upos[:, :, k * V + (1 - a) * HEADS:k * V + (2 - a) * HEADS])
            st.then_inc(s_u, 1)

            def masks5(blk, h):
                dve.wait_ge(arrived[slot(5, blk)][h], uses(5, blk))
                wait(dve, s_s5, blk.at(2, h - 1))
                src = ring[:, slot(5, blk), h * HALF:(h + 1) * HALF, :]
                dve.tensor_scalar(mask5[:, h, 0], src, 0.0, None, ALU.is_gt)
                dve.tensor_scalar(mask5[:, h, 1], src, 0.0, None, ALU.is_lt).then_inc(s_m5, 1)

            def masks_done(blk, h):
                dve.wait_ge(s_m5, blk.at(2, h + 1))
                dve.sem_inc(s_dve, 1)

            def read_logits(blk):
                dve.wait_ge(s_s5, blk.at(2, 2))
                link(dve.tensor_reduce(zz.rearrange("p i h -> p (i h)")[:, 0:6], ST[:, 0:0 + 6], AXX, ALU.add)
                     if False else
                     dve.tensor_reduce(small_e, ST[:, 0:IT * 3 * V].rearrange("p (i k v) -> p i v k", i=IT, k=3),
                                       AXX, ALU.add))
                dve.scalar_tensor_tensor(out=rows(e_f, blk), in0=small_e, scalar=ALPHA, in1=small_e,
                                         op0=ALU.mult, op1=ALU.max).then_inc(s_e5, 1)

            small_e = small[:, 33:45].rearrange("p (i v) -> p i v", i=IT)

            def gru_rows_(n, blk):
                dve.wait_ge(s_sig, n(1))
                link(dve.tensor_tensor(two(gt), E[:, :, 3 * D:4 * D], gates[:, :, 0:D], ALU.mult))
                dve.tensor_tensor(two(gt), E[:, :, 2 * D:3 * D], two(gt), ALU.add).then_inc(s_th, 1)
                dve.wait_ge(s_tn, n(1))
                link(dve.tensor_tensor(two(gt), rows(X, blk), two(gn), ALU.subtract))
                link(dve.tensor_tensor(two(gt), two(gt), gates[:, :, D:2 * D], ALU.mult))

            def step5(mb, eb):
                if mb:
                    masks5(mb, 0)
                if eb:
                    read_logits(eb)
                if mb:
                    masks5(mb, 1)
                    masks_done(mb, 0)
                    masks_done(mb, 1)
                if eb:
                    gru_rows_(lambda k: eb.at(1, k), eb)
                    dve.tensor_tensor(rows(res_eo, eb), two(gt), two(gn), ALU.add).then_inc(s_go, 1)
            q.sweep(step5, 2 * 4)

            dve.wait_ge(s_e5, B)
            dve.wait_ge(s_s5, 2 * B)
            link(dve.tensor_scalar(tmp, e_f[:, :, :], LOG2E, NMAX, ALU.mult, ALU.min))
            link(dve.tensor_scalar(tmp, tmp, -NMAX, ROUND, ALU.max, ALU.add))
            link(dve.tensor_scalar(tmp, tmp, -ROUND, None, ALU.add))
            link(dve.scalar_tensor_tensor(out=nbits[:, :, :], in0=tmp, scalar=-LN2_HI, in1=e_f[:, :, :],
                                          op0=ALU.mult, op1=ALU.add))
            dve.scalar_tensor_tensor(out=nbits[:, :, :], in0=tmp, scalar=-LN2_LO, in1=nbits[:, :, :],
                                     op0=ALU.mult, op1=ALU.add).then_inc(s_ex, 1)
            dve.wait_ge(s_f, 1)
            dve.tensor_scalar(nneg[:, :, :], tmp, -1.0, -SHIFT, ALU.mult, ALU.add)
            link(dve.tensor_scalar(nbits[:, :, :], tmp, 128.0, None, ALU.mult))
            link(dve.tensor_copy(tmp, e_f[:, :, :]))
            three_parts(tmp, lambda k: fpart[:, :, :, k])
            dve.memset(small[:, 33:34], 0.0).then_inc(s_fp, 1)

            dve.wait_ge(s_go, B + 1)

            def maxima(blk):
                for h in range(2):
                    dve.wait_ge(arrived[slot(6, blk)][h], uses(6, blk))
                    src = ring[:, slot(6, blk), h * HALF:(h + 1) * HALF, :]
                    for s, op in ((0, ALU.is_gt), (1, ALU.is_lt)):
                        st = dve.tensor_scalar(mask6[:, s, h * HALF:(h + 1) * HALF, :], src, 0.0, -1.0, op, ALU.mult)
                wait(dve, s_par, blk.at(HEADS))
                link(st)
                link(dve.memset(kmax, 0.0))
                for t in range(T):
                    for s in range(2):
                        for h in range(HEADS):
                            v = s * HEADS + h
                            st = dve.scalar_tensor_tensor(out=kmax[:, h, :], in0=mask6[:, s, t, :],
                                                          scalar=nneg[:, t, v:v + 1], in1=kmax[:, h, :],
                                                          op0=ALU.mult, op1=ALU.max)
                            if t == T - 1 and s == 1:
                                st.then_inc(s_mx, 1)
                        if not (t == T - 1 and s == 1):
                            link(st)

            def spread(blk):
                dve.wait_ge(s_par, blk.at(HEADS, HEADS))
                dve.tensor_scalar(negk, negk, -128.0, 128.0 * (SHIFT + 127.0), ALU.mult, ALU.add).then_inc(s_nk, 1)

            def weigh(blk):
                for c in range(2 * V):
                    v, half = divmod(c, 2)
                    tiles = slice(half * HALF, (half + 1) * HALF)
                    dve.wait_ge(s_t, blk.at(2 * V, c + 1))
                    dve.tensor_tensor(pow_i[:, c % 2], pow_i[:, c % 2], mask6[:, v // HEADS, tiles, :],
                                      ALU.bitwise_and).then_inc(s_tm, 1)
                    dve.wait_ge(s_tm, blk.at(2 * V, c + 1))
                    for t in range(HALF):
                        tt = half * HALF + t
                        st = dve.scalar_tensor_tensor(out=weight[:, c % 2, t, :], in0=ring[:, slot(6, blk), tt, :],
                                                      scalar=e_f[:, tt, v:v + 1], in1=pow_b[:, c % 2, t, :],
                                                      op0=ALU.mult, op1=ALU.mult)
                    st.then_inc(s_w, 1)
                dve.wait_ge(s_w, blk.at(2 * V, 2 * V))
                dve.sem_inc(s_dve, 1)
                dve.sem_inc(s_dve, 1)

            es_rows = xt_es[:, :].rearrange("p (t f) -> p t f", t=T)

            def sum_heads(blk):
                dve.wait_ge(s_tr, blk.at(1, 1))
                link(dve.tensor_reduce(zz, ST[:, 0:IT * 9].rearrange("p (i h k) -> p i h k", i=IT, h=HEADS),
                                       AXX, ALU.add))
                link(dve.tensor_scalar(zz, zz, TINY, float(HEADS), ALU.max, ALU.mult))
                link(dve.reciprocal(rz, zz))
                for h in range(HEADS):
                    for i in range(IT):
                        dst = xt_es[:, bass.ds(blk.at(W, i * D), D)]
                        src = two(hsum[h])[:, i, :]
                        if h == 0:
                            st = dve.tensor_scalar(dst, src, rz[:, i, h:h + 1], None, ALU.mult)
                        else:
                            st = dve.scalar_tensor_tensor(out=dst, in0=src, scalar=rz[:, i, h:h + 1], in1=dst,
                                                          op0=ALU.mult, op1=ALU.add)
                    if h < HEADS - 1:
                        link(st)
                st.then_inc(s_es, 1)

            def step6(mb, eb):
                if mb:
                    maxima(mb)
                if eb:
                    sum_heads(eb)
                if mb:
                    spread(mb)
                    weigh(mb)
            q.sweep(step6, 2 * (2 + 2 * T - 1 + 5))

            def step7(_, blk):
                if not blk:
                    return
                gru_rows_(lambda k: blk.at(1, B + k), blk)
                dve.tensor_tensor(two(gt), two(gt), two(gn), ALU.add).then_inc(s_go, 1)
                dve.wait_ge(s_go, g(1, blk, 1, 2))
                link(dve.tensor_tensor(two(gt), two(gt), rows(res_eo, blk), ALU.add))
                for i in range(IT):
                    xi = X[:, bass.ds(blk.at(IT, i), 1), :].rearrange("p i f -> p (i f)")
                    st = dve.scalar_tensor_tensor(out=xi, in0=two(gt)[:, i, :], scalar=col(dg, blk, i), in1=xi,
                                                  op0=ALU.mult, op1=ALU.add)
                link(st)
                alone(dve)
                for i in range(IT):
                    xi = X[:, bass.ds(blk.at(IT, i), 1), :].rearrange("p i f -> p (i f)")
                    st = dve.bn_stats(bs[:, i, :], xi)
                link(st)
                alone(dve)
                for i in range(IT):
                    st = dve.bn_aggr(mv[:, i, :], bs[:, i, :])
                link(st)
                alone(dve)
                link(dve.tensor_copy(rows(norm, blk), mv))
            q.sweep(step7, 2 * 8)
            dve.tensor_copy(e_f[:, :, 0], norm[:, :, 0]).then_inc(s_var, 1)
            dve.wait_ge(s_std, vbase[5] + 1)
            link(dve.reciprocal(e_f[:, :, 1], norm[:, :, 0]))
            for t in range(T):
                st = dve.tensor_scalar(res_eo[:, t, :], X[:, t, :], e_f[:, t, 0:1], e_f[:, t, 1:2],
                                       ALU.subtract, ALU.mult)
            st.then_inc(s_fin, 1)


def kernel(x, adj, L0_gnn_W, L1_gnn_W1, L1_gnn_b1, L1_gnn_W2, L1_gnn_b2, L1_gnn_W3, L1_gnn_b3,
           L1_gnn_g1, L1_gnn_be1, L1_gnn_g2, L1_gnn_be2, L1_gnn_g3, L1_gnn_be3,
           L2_gnn_weight, L2_gnn_bias, L3_gnn_gat_W, L3_gnn_gat_a,
           L3_gnn_edge_Wih, L3_gnn_edge_Whh, L3_gnn_edge_bih, L3_gnn_edge_bhh,
           L3_gnn_node_Wih, L3_gnn_node_Whh, L3_gnn_node_bih, L3_gnn_node_bhh):
    import numpy as np
    import concourse.bacc as bacc
    from concourse.bass_utils import run_bass_kernel_spmd

    def arr(a):
        return np.asarray(a)

    x, adj = arr(x), arr(adj)
    NP_ = T * P
    off = np.zeros((NP_, NP_), np.float32)
    off[:N, :N] = adj.T
    node = np.arange(NP_)
    off[node, node] = 0.0
    dgn = np.ones(NP_, np.float32)
    dgn[:N] = adj[np.arange(N), np.arange(N)]
    xp = np.zeros((NP_, D), np.float32)
    xp[:N] = x
    a = arr(L3_gnn_gat_a)[:, :, 0].reshape(HEADS, 2, D)
    gw = arr(L3_gnn_gat_W)

    def wide(v):
        return np.broadcast_to(arr(v), (P, D))
    w0 = arr(L0_gnn_W)
    consts = np.concatenate(
        [w0[:, :D].T, w0[:, D:].T, arr(L1_gnn_W1), arr(L1_gnn_W2), arr(L1_gnn_W3), arr(L2_gnn_weight),
         gw.transpose(1, 0, 2).reshape(D, -1), gw.transpose(2, 0, 1).reshape(D, -1),
         a.transpose(2, 0, 1).reshape(D, V)]
        + [wide(v) for v in (L1_gnn_g1, L1_gnn_be1, L1_gnn_g2, L1_gnn_be2, L1_gnn_g3, L1_gnn_be3, L2_gnn_bias)],
        axis=1)
    rows = np.concatenate([arr(v) for v in (L1_gnn_b1, L1_gnn_b2, L1_gnn_b3, L3_gnn_edge_bih, L3_gnn_edge_bhh)])
    arrays = {
        "adjt": off.reshape(T, P, B, W).transpose(2, 1, 0, 3),
        "diag": dgn.reshape(T, P).T,
        "xrow": xp.reshape(T, P, D).transpose(1, 0, 2).reshape(P, T * D),
        "xcol": xp.T,
        "consts": consts,
        "rows": rows[None],
        "gru": np.stack([np.concatenate([arr(i).T, arr(h).T], axis=1) for i, h in
                         ((L3_gnn_edge_Wih, L3_gnn_edge_Whh), (L3_gnn_node_Wih, L3_gnn_node_Whh))]),
        "gru_rows": np.concatenate([arr(L3_gnn_node_bih), arr(L3_gnn_node_bhh)])[None],
        "ident": np.eye(P, dtype=np.float32),
    }
    arrays = {k: np.ascontiguousarray(v) for k, v in arrays.items()}
    nc = bacc.Bacc("TRN2", target_bir_lowering=False, num_devices=1)
    args = {k: nc.dram_tensor(k + "_dram", v.shape, F32, kind="ExternalInput").ap() for k, v in arrays.items()}
    out = nc.dram_tensor("out_dram", (NP_, D), F32, kind="ExternalOutput").ap()
    build(nc, out=out, **args)
    r = run_bass_kernel_spmd(nc, [{k + "_dram": v for k, v in arrays.items()}], core_ids=[0])
    return r.results[0]["out_dram"][:N]
```

```python
from contextlib import ExitStack

import concourse.bass as bass
from concourse import mybir

ALU = mybir.AluOpType
ACT = mybir.ActivationFunctionType
F32 = mybir.dt.float32
BF16 = mybir.dt.bfloat16
I16 = mybir.dt.int16
AXX = mybir.AxisListType.X

N = 3327
P = 128
D = 128
T = -(-N // P)
W = 256
B = T * P // W
IT = W // P
HALF = T // 2
HEADS = 3
V = 2 * HEADS
EPS = 1e-5
ALPHA = 0.2
LOG2E = 1.4426950408889634
LN2_HI = 0.693359375
LN2_LO = -2.12194440e-4
ROUND = 12582912.0
STEP = 16
MSHIFT = 2 ** 14
NMAX = float(STEP * (MSHIFT - 1))
TINY = 1e-30

C_WAB, C_W1, C_W4, C_GW, C_GWT, C_GA = 0, 256, 640, 768, 1152, 1536
C_GB = C_GA + 6
C_END = C_GB + 7 * D
R_B, R_BIH, R_BHH, R_END = 0, 384, 768, 1152

class Block:

    def __init__(self, c, r=0):
        self.c, self.r = c, r

    def at(self, k, base=0):
        return self.r * (2 * k) + (base + k * self.c)

    def cols(self, k):
        return bass.ds(self.at(k), k)


def sweep(eng, step):
    step(Block(0), None)
    with eng.Fori(0, (B - 1) // 2) as r:
        step(Block(1, r), Block(0, r))
        step(Block(2, r), Block(1, r))
    step(None, Block(B - 1))


def sweep_three(eng, step, turn=lambda r: None):
    step(Block(0), None, None)
    step(Block(1), Block(0), None)
    with eng.Fori(0, (B - 3) // 2) as r:
        turn(r)
        step(Block(2, r), Block(1, r), Block(0, r))
        step(Block(3, r), Block(2, r), Block(1, r))
    turn(0)
    step(Block(B - 1), Block(B - 2), Block(B - 3))
    step(None, Block(B - 1), Block(B - 2))
    step(None, None, Block(B - 1))


def build(nc, adjt, diag, xrow, xcol, consts, rows, gru, gru_rows, ident, edge_gru, out):
    ctx = ExitStack()
    with ctx:
        def sb(name, shape, dt=F32):
            return ctx.enter_context(nc.sbuf_tensor(name, shape, dt))

        def sem(name):
            return ctx.enter_context(nc.semaphore(name))

        ring = sb("ring", [P, 2, T, W])
        X = sb("X", [P, T, D])
        res_eo = sb("res_eo", [P, T, D])
        xt_es = sb("xt_es", [P, T * D])
        FW = sb("FW", [P, 2, T * D])
        HW = sb("HW", [P, T, HEADS * D])
        region_m = sb("region_m", [P, T * W])
        region_t = sb("region_t", [P, T * D])
        stage = sb("stage", [P, 2048])
        idn = sb("idn", [P, P])
        ones = sb("ones", [P, P])
        dg = sb("dg", [P, T])
        norm = sb("norm", [P, T, 2])
        small = sb("small", [P, 80])
        e_f = sb("e_f", [P, T, V])
        nbits = sb("nbits", [P, T, V])
        nneg = sb("nneg", [P, T, V])
        fpart = sb("fpart", [P, T, V, 3], BF16)

        cst = region_m[:, 0:C_END]
        wab = cst[:, C_WAB:C_WAB + 2 * D]
        gat_w = cst[:, C_GW:C_GW + HEADS * D]
        gat_wt = cst[:, C_GWT:C_GWT + HEADS * D]
        gat_a = cst[:, C_GA:C_GA + V]
        wa = region_m[:, C_END:C_END + V]

        def gb(k):
            return cst[:, C_GB + k * D:C_GB + (k + 1) * D]

        brow = region_t[0:1, 0:R_END]
        wih = region_t[:, R_END:R_END + 3 * D]
        whh = region_t[:, R_END + 3 * D:R_END + 6 * D]
        o = R_END + 6 * D
        xts = region_t[:, o:o + W]
        colsum = region_t[:, o + W:o + 3 * W].rearrange("p (h c) -> p h c", h=2)
        o += 3 * W
        uraw = region_t[:, o:o + T * V].rearrange("p (t v) -> p t v", v=V)
        o += T * V
        upos = region_t[:, o:o + T * 9].bitcast(BF16).rearrange("p (t k) -> p t k", k=3 * V)
        o += T * 9
        uneg = region_t[:, o:o + T * 9].bitcast(BF16).rearrange("p (t k) -> p t k", k=3 * V)
        assert o + T * 9 <= T * D

        mask5 = region_m[:, :].bitcast(BF16).rearrange("p (h s t c) -> p h s t c", h=2, s=2, t=HALF)
        mask6 = region_m[:, :].bitcast(I16).rearrange("p (k t c) -> p k t c", k=2, t=T)
        cand = res_eo[:, :, :].rearrange("p t f -> p (t f)").bitcast(I16)\
            .rearrange("p (k t c) -> p k t c", k=2, t=HALF)
        eo7 = region_m[:, 0:T * D].rearrange("p (t f) -> p t f", t=T)
        dump = HW[:, :, :].rearrange("p t f -> p (t f)")[:, 0:HALF * W].rearrange("p (t c) -> p t c", t=HALF)
        pow_i = region_t[:, :].bitcast(I16).rearrange("p (k t c) -> p k t c", k=2, t=HALF)
        pow_b = region_t[:, :].bitcast(BF16).rearrange("p (k t c) -> p k t c", k=2, t=HALF)
        weight = FW[:, :, :].rearrange("p k (t c) -> p k t c", t=HALF)

        def stg(k):
            return stage[:, k * W:(k + 1) * W]
        xs, zs, xTs, ys, gn, gt = (stg(k) for k in (0, 1, 2, 3, 6, 7))
        gates = stage[:, 4 * W:6 * W].rearrange("p (i c) -> p i c", i=IT)
        kmax = stage[:, 0:3 * W // 2].bitcast(I16).rearrange("p (h c) -> p h c", h=HEADS)
        kneg = stage[:, 3 * W // 2:2 * W].bitcast(I16)
        negk = stage[:, 2 * W:5 * W].rearrange("p (h c) -> p h c", h=HEADS)
        heads_t = stage[:, 5 * W:8 * W].rearrange("p (h c) -> p h c", h=HEADS)

        def two(ap):
            return ap.rearrange("p (i f) -> p i f", i=IT)

        sd = small[:, 0:4].rearrange("p (i k) -> p i k", i=IT)
        rec = small[:, 4:6]
        drec = small[:, 6:8]
        bs = small[:, 8:20].rearrange("p (i k) -> p i k", i=IT)
        mv = small[:, 20:24].rearrange("p (i k) -> p i k", i=IT)
        std = small[:, 24:28]
        rstd = small[:, 28:30]
        eps = small[:, 30:31]
        diag1 = small[:, 31:33]
        zz = small[:, 33:39].rearrange("p (i h) -> p i h", i=IT)
        rz = small[:, 39:45].rearrange("p (i h) -> p i h", i=IT)
        small_e = small[:, 33:45].rearrange("p (i v) -> p i v", i=IT)
        cell = small[:, 45:46]
        negsum = small[:, 48:48 + T]
        negtot, negall = small[:, 74:75], small[:, 75:76]
        flag = small[:, 76:77].bitcast(mybir.dt.int32)

        def ps(name, banks=1):
            return ctx.enter_context(nc.psum_tensor(name, [P, 512 * banks], F32))
        Z = [ps("Z0"), ps("Z1")]
        TP, HB, HC, ST = ps("TP"), ps("HB"), ps("HC"), ps("ST")
        E = ps("E", 2).rearrange("p (i c) -> p i c", i=IT)
        NUMB = [(Z[0], Z[1]), (E[:, 0, :], E[:, 1, :])]
        tp, hb, hc = (x[:, 0:W] for x in (TP, HB, HC))
        DEN = [ST, TP]
        hsum = [hb, HB[:, W:2 * W], hc]
        GATE = [E, (Z[0], Z[1])]

        s_c = sem("constants_in")
        s_x = sem("x_in")
        s_g = sem("edge_weights_in")
        s_n = sem("node_weights_in")
        arrived = [[sem(f"arrived_{s}{h}") for h in range(2)] for s in range(2)]
        s_init = sem("init_done")
        s_pe = sem("pe_half_done")
        s_dve = sem("dve_half_done")
        s_wa = sem("wa_product")
        s_was = sem("wa_stored")
        s_zs = sem("zs_ready")
        s_a = sem("closing_a_done")
        s_var = sem("to_sqrt")
        s_std = sem("sqrt_done")
        s_d1 = sem("rows_ready")
        s_b = sem("rows_transposed")
        s_xt = sem("xTs_ready")
        s_cc = sem("closing_c_done")
        s_d2 = sem("operand_ready")
        s_u = sem("u_parts_ready")
        s_m5 = sem("sign_masks_ready")
        s_s5 = sem("logits_half_done")
        s_e5 = sem("logits_read")
        s_sig = sem("sigmoid_done")
        s_th = sem("to_tanh")
        s_tn = sem("tanh_done")
        s_go = sem("gru_done")
        s_ex = sem("to_exp")
        s_f = sem("exp_done")
        s_fp = sem("f_parts_ready")
        s_neg = sem("negatives_summed")
        s_nt = sem("negatives_total")
        s_na = sem("negatives_reduced")
        s_flag = sem("flag_ready")
        s_eos = sem("edge_gru_stored")
        s_mk = sem("mask_half_ready")
        s_cd = sem("candidates_ready")
        s_tree = sem("candidates_reduced")
        s_mx = sem("max_ready")
        s_par = sem("max_reduced")
        s_nk = sem("negk_ready")
        s_t = sem("powers_ready")
        s_tm = sem("powers_masked")
        s_w = sem("weights_ready")
        s_c6 = sem("chunk_done")
        s_t2 = sem("neg_powers_ready")
        s_tm2 = sem("neg_powers_masked")
        s_w2 = sem("neg_weights_ready")
        s_c2 = sem("neg_chunk_done")
        s_q2 = sem("dve_neg_chain")
        s_q3 = sem("neg_powers_finite")
        s_ev = sem("heads_copied")
        s_tr = sem("heads_transposed")
        s_es = sem("heads_summed")
        s_q = sem("dve_chain")
        s_qa = sem("act_chain")
        s_out = sem("out_written")
        s_fin = sem("final_rows")

        ACT_CHUNKS = (0, 1, 3, 4)
        NEG_LINKS = T * HEADS * 3
        VAR = [2, 1, 1, 2, 1]
        vbase = [B * sum(VAR[:p]) for p in range(6)]

        def wait(eng, semaphore, value):
            if not (isinstance(value, int) and value <= 0):
                eng.wait_ge(semaphore, value)

        def alone(eng):
            eng.nop(nofuse=True)

        class Links:

            def __init__(self, eng, semaphore):
                self.eng, self.sem = eng, semaphore
                self.done, self.turn = 0, 0

            def link(self, ins):
                ins.then_inc(self.sem, 1)
                self.done += 1
                self.eng.wait_ge(self.sem, self.turn + self.done)

            def sweep(self, step, per):
                step(Block(0), None)
                before = self.done
                with self.eng.Fori(0, (B - 1) // 2) as r:
                    self.turn = r * per
                    step(Block(1, r), Block(0, r))
                    step(Block(2, r), Block(1, r))
                self.turn = 0
                assert self.done - before == per, (self.done - before, per)
                self.done = before + per * ((B - 1) // 2)
                step(None, Block(B - 1))

            def sweep_three(self, step, per):
                def turn(r):
                    if isinstance(r, int):
                        self.turn = 0
                        assert self.done - self.before == per, (self.done - self.before, per)
                        self.done = self.before + per * ((B - 3) // 2)
                    else:
                        self.before = self.done
                        self.turn = r * per
                sweep_three(self.eng, step, turn)

        def slot(p, blk):
            return (p * B + blk.c) % 2

        def uses(p, blk, k=0):
            return blk.r * 16 + 16 * ((p * B + blk.c) // 2 + 1)

        def g(p, blk, k, more=0):
            return blk.at(k, k * p * B + more)

        block = ctx.enter_context(nc.Block())

        @block.sync
        def _(sp):
            sp.dma_start(cst, consts).then_inc(s_c, 16)
            sp.dma_start(FW[:, 0, :], xrow).then_inc(s_x, 16)
            sp.dma_start(xt_es[:, :], xcol).then_inc(s_x, 16)
            sp.dma_start(dg[:, :], diag).then_inc(s_c, 16)
            sp.dma_start(idn[:, :], ident).then_inc(s_c, 16)
            sp.dma_start(brow, rows).then_inc(s_c, 16)
            sp.dma_start(region_t[:, R_END:R_END + 6 * D], gru[0]).then_inc(s_g, 16)

            def load(p, blk, pe_wait=None, dve_wait=None):
                for h in range(2):
                    if pe_wait is not None:
                        sp.wait_ge(s_pe, pe_wait(h))
                    if dve_wait is not None:
                        alone(sp)
                        sp.wait_ge(*dve_wait(h))
                    src = adjt[bass.ds(blk.at(1), 1), :, h * HALF:(h + 1) * HALF, :]
                    sp.dma_start(ring[:, slot(p, blk), h * HALF:(h + 1) * HALF, :],
                                 src.rearrange("a p t c -> (a p) t c"))\
                        .then_inc(arrived[slot(p, blk)][h], 16)

            DB = {0: (s_dve, 0), 1: (s_neg, 0), 5: (s_m5, 0), 6: (s_dve, 2 * B)}
            for p in range(7):
                def pe_wait(blk):
                    if p == 6:
                        return None
                    return lambda h: g(p, blk, 2, h - 3)

                def dve_wait(blk):
                    if p not in DB:
                        return None
                    return lambda h: (DB[p][0], blk.at(2, DB[p][1] + h - 3))

                for c in range(2):
                    if p == 0:
                        load(p, Block(c))
                    elif p == 6:
                        load(p, Block(c), lambda h: 2 * 6 * B, lambda h: (s_m5, 2 * B))
                    elif p == 5:
                        load(p, Block(c), pe_wait(Block(c)))
                    else:
                        load(p, Block(c), pe_wait(Block(c)),
                             {1: lambda h: (s_dve, 2 * B), 2: lambda h: (s_neg, 2 * B)}.get(p))
                with sp.Fori(0, (B - 3) // 2) as r:
                    load(p, Block(2, r), pe_wait(Block(2, r)), dve_wait(Block(2, r)))
                    load(p, Block(3, r), pe_wait(Block(3, r)), dve_wait(Block(3, r)))
                last = Block(B - 1)
                load(p, last, pe_wait(last), dve_wait(last))
            sp.wait_ge(s_es, B + 1)
            sp.wait_ge(s_eos, 16)
            sp.dma_start(eo7, edge_gru).then_inc(s_n, 16)
            sp.dma_start(region_t[0:1, 0:6 * D], gru_rows).then_inc(s_n, 16)
            sp.dma_start(region_t[:, R_END:R_END + 6 * D], gru[1]).then_inc(s_n, 16)
            sp.wait_ge(s_fin, 1)
            sp.dma_start(out.rearrange("(t p) f -> p t f", p=P), res_eo[:, :, :]).then_inc(s_out, 16)
            sp.wait_ge(s_out, 16)

        @block.tensor
        def _(pe):
            pe.wait_ge(s_c, 64)
            pe.wait_ge(s_g, 16)
            pe.wait_ge(s_init, 4)
            for h in range(HEADS):
                last = pe.matmul(ST[:, 2 * h:2 * h + 2], gat_wt[:, h * D:(h + 1) * D],
                                 gat_a[:, 2 * h:2 * h + 2], start=True, stop=True)
            last.then_inc(s_wa, 1)
            pe.wait_ge(s_x, 32)

            def main(p, blk, t0, t1):
                zz_ = Z[slot(p, blk)][:, 0:W]
                for t in range(t0, t1):
                    if t in (0, HALF):
                        pe.wait_ge(arrived[slot(p, blk)][t // HALF], uses(p, blk))
                    f = X[:, t, :] if p == 5 else FW[:, p % 2, t * D:(t + 1) * D]
                    mm = pe.matmul(zz_, f, ring[:, slot(p, blk), t, :], start=t == 0, stop=t == T - 1)
                    if t in (HALF - 1, T - 1):
                        mm.then_inc(s_pe, 1)

            def step_a(p, blk):
                pe.wait_ge(s_zs, g(p, blk, 1, 1))
                if p == 0:
                    pe.wait_ge(s_dve, blk.at(2, 2))
                    for i in range(IT):
                        s = slice(i * P, (i + 1) * P)
                        pe.matmul(E[:, i, 0:2 * D], xts[:, s], wab, start=True, stop=True)
                        pe.matmul(E[:, i, 2 * D:3 * D], zs[:, s], wab[:, D:2 * D], start=True, stop=True)
                        pe.matmul(E[:, i, 3 * D:3 * D + 1], colsum[:, 0, s], ones[:, 0:1], start=True, stop=False)
                        last = pe.matmul(E[:, i, 3 * D:3 * D + 1], colsum[:, 1, s], ones[:, 0:1],
                                         start=False, stop=True)
                    last.then_inc(s_a, 1)
                else:
                    for i in range(IT):
                        last = pe.transpose(two(tp)[:, i, :], zs[:, i * P:(i + 1) * P], idn[:, :])
                    last.then_inc(s_a, 1)

            def step_b(p, blk):
                pe.wait_ge(s_d1, g(p, blk, 1, 1))
                for i in range(IT):
                    last = pe.transpose(two(hb)[:, i, :], xs[:, i * P:(i + 1) * P], idn[:, :])
                last.then_inc(s_b, 1)

            def step_c(p, blk):
                if p == 3:
                    wgt = cst[:, C_W4:C_W4 + D]
                elif p < 3:
                    wgt = cst[:, C_W1 + p * D:C_W1 + (p + 1) * D]
                pe.wait_ge(s_xt, g(p, blk, 1, 1))
                for i in range(IT):
                    lhs = xTs[:, i * P:(i + 1) * P]
                    if p == 4:
                        pe.matmul(E[:, i, 0:3 * D], lhs, gat_w, start=True, stop=True)
                        last = pe.matmul(E[:, i, 3 * D:3 * D + V], lhs, wa, start=True, stop=True)
                    else:
                        last = pe.matmul(two(hc)[:, i, :], lhs, wgt, start=i == 0, stop=p == 3,
                                         skip_group_check=True)
                        if p < 3:
                            last = pe.matmul(two(hc)[:, i, :], ones[0:1, :],
                                             brow[:, R_B + p * D:R_B + (p + 1) * D],
                                             start=False, stop=True, skip_group_check=True)
                last.then_inc(s_cc, 1)

            pe.wait_ge(s_was, 1)

            def step(p, mb, eb):
                main(p, mb, 0, 9)
                step_a(p, eb)
                main(p, mb, 9, 18)
                step_b(p, eb)
                main(p, mb, 18, T)
                step_c(p, eb)

            def seam(p):
                mb, eb = Block(0), Block(B - 1)
                pe.wait_ge(s_d2, p * B + B - 1)
                main(p + 1, mb, 0, 9)
                step_a(p, eb)
                main(p + 1, mb, 9, 18)
                step_b(p, eb)
                main(p + 1, mb, 18, T - IT)
                step_c(p, eb)
                pe.wait_ge(s_d2, (p + 1) * B)
                main(p + 1, mb, T - IT, T)

            main(0, Block(0), 0, T)
            for p in range(5):
                with pe.Fori(0, (B - 1) // 2) as r:
                    step(p, Block(1, r), Block(0, r))
                    step(p, Block(2, r), Block(1, r))
                seam(p)

            def gru_products(bias, E):
                for i in range(IT):
                    s = slice(i * P, (i + 1) * P)
                    pe.matmul(E[i][:, 0:3 * D], zs[:, s], wih, start=True, stop=False, skip_group_check=True)
                    pe.matmul(E[i][:, 0:2 * D], xTs[:, s], whh[:, 0:2 * D], start=False, stop=False,
                              skip_group_check=True)
                    pe.matmul(E[i][:, 3 * D:4 * D], xTs[:, s], whh[:, 2 * D:3 * D], start=False, stop=False,
                              skip_group_check=True)
                    pe.matmul(E[i][:, 0:3 * D], ones[0:1, :], bias[:, 0:3 * D], start=False, stop=False,
                              skip_group_check=True)
                    pe.matmul(E[i][:, 0:2 * D], ones[0:1, :], bias[:, 3 * D:5 * D], start=False, stop=True,
                              skip_group_check=True)
                    last = pe.matmul(E[i][:, 3 * D:4 * D], ones[0:1, :], bias[:, 5 * D:6 * D],
                                     start=False, stop=True, skip_group_check=True)
                last.then_inc(s_cc, 1)

            def logits(blk, h):
                pe.wait_ge(s_m5, blk.at(2, h + 1))
                if h == 0:
                    wait(pe, s_e5, blk.at(1))
                for t in range(HALF):
                    for i in range(IT):
                        for s, u in ((0, upos), (1, uneg)):
                            first = h == 0 and t == 0 and i == 0 and s == 0
                            last = pe.matmul(ST[:, i * 3 * V:(i + 1) * 3 * V],
                                             mask5[:, h, s, t, i * P:(i + 1) * P], u[:, h * HALF + t, :],
                                             start=first, stop=h == 1 and t == HALF - 1 and s == 1,
                                             skip_group_check=True)
                last.then_inc(s_s5, 1)

            def step5(mb, eb):
                if mb and mb.c:
                    main(5, mb, 0, HALF)
                if eb:
                    step_b(5, eb)
                if mb:
                    logits(mb, 0)
                    if mb.c:
                        main(5, mb, HALF, T)
                if eb:
                    pe.wait_ge(s_zs, g(5, eb, 1, 1))
                    pe.wait_ge(s_xt, g(5, eb, 1, 1))
                    gru_products(brow[:, R_BIH:R_END], [E[:, i, :] for i in range(IT)])
                if mb:
                    logits(mb, 1)
            pe.wait_ge(s_u, 1)
            sweep(pe, step5)

            pe.wait_ge(s_fp, 1)
            pe.wait_ge(s_zs, 6 * B)
            pe.wait_ge(s_flag, 1)
            any_negative = pe.value_load(flag[0:1, 0:1], min_val=0, max_val=1)

            def products(blk, half, v, buf, masked, weighed, first):
                par, h = blk.c % 2, v % HEADS
                pe.wait_ge(*masked)
                for t in range(HALF):
                    for i in range(IT):
                        k = i * 9 + h * 3
                        pe.matmul(DEN[par][:, k:k + 3], pow_b[:, buf, t, i * P:(i + 1) * P],
                                  fpart[:, half * HALF + t, v, :],
                                  start=first and h == 0 and t == 0 and i == 0,
                                  stop=half == 1 and t == HALF - 1, skip_group_check=True)
                pe.wait_ge(*weighed)
                for t in range(HALF):
                    last = pe.matmul(NUMB[par][h // 2][:, h % 2 * W:(h % 2 + 1) * W],
                                     HW[:, half * HALF + t, h * D:(h + 1) * D], weight[:, buf, t, :],
                                     start=first and h % 2 == 0 and t == 0,
                                     stop=half == 1 and t == HALF - 1, skip_group_check=True)
                return last

            def step6(_, wb, sb_):
                for c in range(V):
                    half, h = divmod(c, HEADS)
                    if wb:
                        if c == 0:
                            wait(pe, s_es, wb.at(1) if wb.c else 0)
                        products(wb, half, h, c % 2, (s_tm, wb.at(V, c + 1)), (s_w, wb.at(V, c + 1)), half == 0)\
                            .then_inc(s_c6, 1)
                        if c % HEADS == HEADS - 1:
                            with pe.If(any_negative):
                                for n in range(HEADS):
                                    k = wb.at(V, half * HEADS + n + 1)
                                    products(wb, half, HEADS + n, 0, (s_tm2, k), (s_w2, k), False)\
                                        .then_inc(s_c2, 1)
                    if sb_ and c == 1:
                        pe.wait_ge(s_ev, sb_.at(1, 1))
                        alone(pe)
                        pe.wait_ge(s_es, sb_.at(1, 1))
                        for n in range(HEADS):
                            for i in range(IT):
                                last = pe.transpose(two(hsum[n])[:, i, :], heads_t[:, n, i * P:(i + 1) * P],
                                                    idn[:, :])
                        last.then_inc(s_tr, 1)
            sweep_three(pe, step6)

            pe.wait_ge(s_n, 48)
            pe.wait_ge(s_es, B + 1)

            def step7(mb, eb):
                if mb:
                    pe.wait_ge(s_d1, g(6, mb, 1, 1))
                    for i in range(IT):
                        pe.transpose(two(hb)[:, i, :], xs[:, i * P:(i + 1) * P], idn[:, :])
                    for i in range(IT):
                        last = pe.transpose(two(tp)[:, i, :], ys[:, i * P:(i + 1) * P], idn[:, :])
                    last.then_inc(s_b, 1)
                if mb:
                    pe.wait_ge(s_xt, g(6, mb, 1, 1))
                    gate = GATE[mb.c % 2]
                    gru_products(region_t[0:1, 0:6 * D],
                                 [gate[:, i, :] for i in range(IT)] if mb.c % 2 == 0 else list(gate))
            sweep(pe, step7)

        @block.scalar
        def _(act):
            act.wait_ge(s_x, 32)
            act.wait_ge(s_init, 4)
            act.wait_ge(s_wa, 1)
            act.activation(wa.rearrange("p (k h) -> p h k", k=2),
                           ST[:, 0:V].rearrange("p (h k) -> p h k", k=2), ACT.Copy).then_inc(s_was, 1)

            def copy_z(p, blk):
                act.wait_ge(s_pe, g(p, blk, 2, 2))
                if p == 0:
                    act.activation(xts, xt_es[:, blk.cols(W)], ACT.Copy)
                act.activation(zs, Z[slot(p, blk)][:, 0:W], ACT.Copy).then_inc(s_zs, 1)

            def copy_xt(p, blk):
                act.wait_ge(s_b, g(p, blk, 1, 1))
                act.activation(xTs, hb, ACT.Copy).then_inc(s_xt, 1)

            for p in range(5):
                def negatives(blk, h):
                    act.wait_ge(arrived[slot(1, blk)][h], uses(1, blk))
                    alone(act)
                    wait(act, s_neg, blk.at(2, h))
                    alone(act)
                    act.activation(dump, ring[:, slot(1, blk), h * HALF:(h + 1) * HALF, :], ACT.Relu, scale=-1.0,
                                   accum_out=negsum[:, bass.ds(blk.at(2, h), 1)]).then_inc(s_neg, 1)

                def step(mb, eb):
                    if p == 1 and mb:
                        negatives(mb, 0)
                        if not eb:
                            negatives(mb, 1)
                    if not eb:
                        return
                    copy_z(p, eb)
                    if p == 0:
                        act.wait_ge(s_var, eb.at(2, 1))
                        act.activation(std[:, 0:4], small[:, 0:4], ACT.Sqrt).then_inc(s_std, 1)
                    for k in range(1 if p == 0 else 0, VAR[p]):
                        act.wait_ge(s_var, eb.at(VAR[p], vbase[p] + k + 1))
                        act.activation(std[:, 0:2], mv[:, :, 1], ACT.Sqrt, bias=eps).then_inc(s_std, 1)
                    copy_xt(p, eb)
                    if p == 1 and mb:
                        negatives(mb, 1)
                sweep(act, step)

            def gate_functions(n, E):
                act.wait_ge(s_cc, n(1 + 5 * B))
                alone(act)
                act.wait_ge(s_go, n(1))
                act.activation(gates[:, :, :], E[:, :, 0:2 * D], ACT.Sigmoid).then_inc(s_sig, 1)
                act.wait_ge(s_th, n(1))
                act.activation(gn, gt, ACT.Tanh).then_inc(s_tn, 1)

            def step5(mb, eb):
                if not eb:
                    return
                act.wait_ge(s_cc, g(5, eb, 1))
                act.activation(xs, X[:, eb.cols(IT), :].rearrange("p i f -> p (i f)"), ACT.Copy)\
                    .then_inc(s_d1, 1)
                copy_z(5, eb)
                copy_xt(5, eb)
                gate_functions(lambda k: eb.at(1, k), E)
            sweep(act, step5)

            act.wait_ge(s_ex, 1)
            act.activation(e_f[:, :, :], nbits[:, :, :], ACT.Exp).then_inc(s_f, 1)

            act.wait_ge(s_flag, 1)
            any_negative = act.value_load(flag[0:1, 0:1], min_val=0, max_val=1)
            act.wait_ge(s_fp, 1)
            act.wait_ge(s_eos, 16)

            def powers(half, v, buf):
                for t in range(HALF):
                    tt = half * HALF + t
                    last = act.activation(pow_i[:, buf, t, :], negk[:, v % HEADS, :], ACT.Relu,
                                          bias=nbits[:, tt, v:v + 1])
                return last

            def step6(xb, wb, sb_):
                for c in range(V):
                    half, h = divmod(c, HEADS)
                    if wb:
                        if half == 0:
                            act.wait_ge(s_nk, wb.at(HEADS, h + 1))
                        if c < 2:
                            wait(act, s_c6, wb.at(V, c - 1) if wb.c else 0)
                        else:
                            act.wait_ge(s_c6, wb.at(V, c - 1))
                        powers(half, h, c % 2).then_inc(s_t, 1)
                    if xb and c in ACT_CHUNKS:
                        act.wait_ge(s_mk, xb.at(2, half + 1))
                        alone(act)
                        if c < 2:
                            wait(act, s_tree, xb.at(V, c - 1) if xb.c else 0)
                        else:
                            act.wait_ge(s_tree, xb.at(V, c - 1))
                        for t in range(HALF):
                            tt = half * HALF + t
                            last = act.activation(cand[:, c % 2, t, :], mask6[:, xb.c % 2, tt, :], ACT.Copy,
                                                  scale=nneg[:, tt, h:h + 1])
                        last.then_inc(s_cd, 1)
                    if wb and c % HEADS == HEADS - 1:
                        with act.If(any_negative):
                            act.wait_ge(s_c6, wb.at(V, c + 1))
                            for n in range(HEADS):
                                powers(half, HEADS + n, 0).then_inc(s_t2, 1)
                                act.wait_ge(s_c2, wb.at(V, half * HEADS + n + 1))
                            alone(act)
                    if sb_ and c == 1:
                        act.wait_ge(s_c6, sb_.at(V, V))
                        bank = NUMB[sb_.c % 2]
                        act.activation(stage[:, 5 * W:7 * W], bank[0][:, 0:2 * W], ACT.Copy)
                        act.activation(stage[:, 7 * W:8 * W], bank[1][:, 0:W], ACT.Copy).then_inc(s_ev, 1)
            sweep_three(act, step6)

            act.wait_ge(s_es, B + 1)

            def step7(mb, eb):
                if mb:
                    if mb.c:
                        act.wait_ge(s_b, g(6, mb, 1))
                    act.activation(xs, X[:, mb.cols(IT), :].rearrange("p i f -> p (i f)"), ACT.Copy)
                    act.activation(ys, xt_es[:, mb.cols(W)], ACT.Copy).then_inc(s_d1, 1)
                if eb:
                    gate = E if eb.c % 2 == 0 else None
                    act.wait_ge(s_cc, g(6, eb, 1, 1))
                    alone(act)
                    act.wait_ge(s_go, eb.at(1, B + 1))
                    for i in range(IT):
                        last = act.activation(gates[:, i, :], (gate[:, i, :] if gate is not None else
                                                               GATE[1][i])[:, 0:2 * D], ACT.Sigmoid)
                    last.then_inc(s_sig, 1)
                if mb:
                    act.wait_ge(s_b, g(6, mb, 1, 1))
                    act.activation(zs, tp, ACT.Copy)
                    act.activation(xTs, hb, ACT.Copy).then_inc(s_xt, 1)
                if eb:
                    act.wait_ge(s_th, eb.at(1, B + 1))
                    act.activation(gn, gt, ACT.Tanh).then_inc(s_tn, 1)
            sweep(act, step7)
            act.wait_ge(s_var, vbase[5] + 1)
            act.activation(norm[:, :, 0], norm[:, :, 1], ACT.Sqrt, bias=eps).then_inc(s_std, 1)

        @block.gpsimd
        def _(pool):
            pool.wait_ge(s_nt, 1)
            pool.partition_all_reduce(negall, negtot, P, bass.bass_isa.ReduceOp.add).then_inc(s_na, 1)
            pool.wait_ge(s_go, B + 1)
            pool.dma_start(edge_gru, res_eo[:, :, :]).then_inc(s_eos, 16)

            def spread(blk, _, __):
                if not blk:
                    return
                for h in range(HEADS):
                    wait(pool, s_t, blk.at(V, h + 4 - V))
                    alone(pool)
                    pool.wait_ge(s_mx, blk.at(HEADS, h + 1))
                    alone(pool)
                    pool.partition_all_reduce(negk[:, h, :], kmax[:, h, :], P, bass.bass_isa.ReduceOp.max)\
                        .then_inc(s_par, 1)
                    pool.wait_ge(s_par, blk.at(HEADS, h + 1))
                    alone(pool)
                    pool.tensor_scalar(negk[:, h, :], negk[:, h, :], -128.0 * STEP, 128.0 * (STEP * MSHIFT + 127),
                                       ALU.mult, ALU.add).then_inc(s_nk, 1)
            sweep_three(pool, spread)

        @block.vector
        def _(dve):
            q = Links(dve, s_q)
            link = q.link
            dve.memset(ones[:, :], 1.0).then_inc(s_init, 1)
            dve.memset(eps, EPS).then_inc(s_init, 1)
            dve.memset(rec, 0.0).then_inc(s_go, 1)
            dve.memset(small[:, 31:48], 0.0).then_inc(s_init, 1)
            dve.memset(small[:, 48:80], 0.0).then_inc(s_es, 1)
            dve.memset(colsum, 0.0).then_inc(s_init, 1)
            dve.wait_ge(s_c, 64)
            dve.wait_ge(s_x, 32)
            dve.wait_ge(s_was, 1)

            def layer_norm(y, dst, vwait):
                for i in range(IT):
                    st = dve.bn_stats(bs[:, i, :], two(y)[:, i, :])
                link(st)
                alone(dve)
                for i in range(IT):
                    st = dve.bn_aggr(mv[:, i, :], bs[:, i, :])
                st.then_inc(s_var, 1)
                dve.wait_ge(s_std, vwait)
                link(dve.reciprocal(rstd, std[:, 0:2]))
                for i in range(IT):
                    st = dve.tensor_scalar(two(dst)[:, i, :], two(y)[:, i, :], mv[:, i, 0:1], rstd[:, i:i + 1],
                                           ALU.subtract, ALU.mult)
                link(st)

            def per_row(k):
                return gb(k).rearrange("p (i f) -> p i f", i=1).broadcast_to([P, IT, D])

            def rows(buf, blk):
                return buf[:, blk.cols(IT), :]

            def f_rows(p, blk):
                return FW[:, p % 2, :].rearrange("p (t f) -> p t f", t=T)[:, blk.cols(IT), :]

            def col(ap, blk, i):
                return ap[:, bass.ds(blk.at(IT, i), 1)]

            def sums(blk):
                for h in range(2):
                    dve.wait_ge(arrived[slot(0, blk)][h], uses(0, blk))
                    if h == 0:
                        wait(dve, s_a, blk.at(1))
                    dve.tensor_reduce(colsum[:, h, :],
                                      ring[:, slot(0, blk), h * HALF:(h + 1) * HALF, :]
                                      .rearrange("p t c -> p c t"), AXX, ALU.add).then_inc(s_dve, 1)

            def close0(blk):
                dve.wait_ge(s_a, blk.at(1, 1))
                link(dve.tensor_tensor(sd[:, :, 0:1], E[:, :, 3 * D:3 * D + 1],
                                       dg[:, blk.cols(IT)].rearrange("p (i k) -> p i k", k=1), ALU.add))
                link(dve.tensor_scalar(sd[:, :, 1], sd[:, :, 0], 1.0, None, ALU.add))
                dve.reciprocal(rec, sd[:, :, 1]).then_inc(s_var, 1)
                dve.wait_ge(s_var, blk.at(2, 1))
                link(dve.tensor_tensor(drec, rec, dg[:, blk.cols(IT)], ALU.mult))
                for i in range(IT):
                    st = dve.tensor_scalar(two(ys)[:, i, :], E[:, i, 2 * D:3 * D], rec[:, i:i + 1], None, ALU.mult)
                link(st)
                for i in range(IT):
                    st = dve.scalar_tensor_tensor(out=two(ys)[:, i, :], in0=E[:, i, D:2 * D],
                                                  scalar=drec[:, i:i + 1], in1=two(ys)[:, i, :],
                                                  op0=ALU.mult, op1=ALU.add)
                link(st)
                link(dve.tensor_tensor(two(ys), E[:, :, 0:D], two(ys), ALU.add))
                link(dve.tensor_tensor(two(ys), f_rows(0, blk), two(ys), ALU.add))
                dve.wait_ge(s_std, blk.at(2, 1))
                link(dve.reciprocal(rows(norm, blk).rearrange("p i k -> p (i k)"), std[:, 0:4]))
                layer_norm(ys, xs, blk.at(2, 2))
                alone(dve)
                dve.tensor_copy(rows(X, blk), two(xs)).then_inc(s_d1, 1)

            def close_l(p, blk):
                dve.wait_ge(s_a, g(p, blk, 1, 1))
                for i in range(IT):
                    st = dve.scalar_tensor_tensor(out=two(ys)[:, i, :],
                                                  in0=FW[:, p % 2, bass.ds(blk.at(W, i * D), D)],
                                                  scalar=col(dg, blk, i), in1=two(tp)[:, i, :],
                                                  op0=ALU.mult, op1=ALU.add)
                link(st)
                for i in range(IT):
                    st = dve.tensor_scalar(two(ys)[:, i, :], two(ys)[:, i, :], norm[:, bass.ds(blk.at(IT, i), 1), 0],
                                           0.0, ALU.mult, ALU.max)
                link(st)
                link(dve.tensor_tensor(two(ys), two(ys), rows(res_eo, blk), ALU.add))
                layer_norm(ys, xs, blk.at(VAR[p], vbase[p] + 1))
                link(dve.tensor_tensor(two(xs), two(xs), per_row(2 * p - 2), ALU.mult))
                if p < 3:
                    link(dve.tensor_tensor(two(xs), two(xs), per_row(2 * p - 1), ALU.add))
                    alone(dve)
                    dve.tensor_copy(rows(res_eo, blk), two(xs)).then_inc(s_d1, 1)
                else:
                    link(dve.tensor_tensor(two(xs), two(xs), per_row(2 * p - 1), ALU.add))
                    link(dve.tensor_tensor(two(ys), two(xs), rows(X, blk), ALU.add))
                    layer_norm(ys, xs, blk.at(VAR[p], vbase[p] + 2))
                    alone(dve)
                    dve.tensor_copy(rows(X, blk), two(xs)).then_inc(s_d1, 1)

            def close4(blk):
                dve.wait_ge(s_a, g(4, blk, 1, 1))
                link(dve.tensor_scalar(diag1, dg[:, blk.cols(IT)], 1.0, None, ALU.add))
                for i in range(IT):
                    st = dve.scalar_tensor_tensor(out=two(ys)[:, i, :],
                                                  in0=FW[:, 0, bass.ds(blk.at(W, i * D), D)],
                                                  scalar=diag1[:, i:i + 1], in1=two(tp)[:, i, :],
                                                  op0=ALU.mult, op1=ALU.add)
                link(st)
                for i in range(IT):
                    st = dve.scalar_tensor_tensor(out=two(ys)[:, i, :], in0=two(ys)[:, i, :],
                                                  scalar=norm[:, bass.ds(blk.at(IT, i), 1), 1], in1=gb(6),
                                                  op0=ALU.mult, op1=ALU.add)
                link(st)
                link(dve.tensor_tensor(two(ys), two(ys), rows(X, blk), ALU.add))
                layer_norm(ys, xs, blk.at(1, vbase[4] + 1))
                alone(dve)
                dve.tensor_copy(rows(X, blk), two(xs)).then_inc(s_d1, 1)

            def operand(p, blk):
                dve.wait_ge(s_cc, g(p, blk, 1, 1))
                if p == 4:
                    alone(dve)
                    dve.tensor_copy(rows(HW, blk), E[:, :, 0:3 * D])
                    alone(dve)
                    dve.tensor_copy(rows(uraw, blk), E[:, :, 3 * D:3 * D + V]).then_inc(s_d2, 1)
                    return
                if p == 0:
                    alone(dve)
                    dve.tensor_copy(rows(res_eo, blk), two(hc))
                for i in range(IT):
                    st = dve.tensor_scalar(FW[:, (p + 1) % 2, bass.ds(blk.at(W, i * D), D)], two(hc)[:, i, :],
                                           norm[:, bass.ds(blk.at(IT, i), 1), 1 if p == 3 else 0], None, ALU.mult)
                st.then_inc(s_d2, 1)

            close = [close0, lambda b: close_l(1, b), lambda b: close_l(2, b), lambda b: close_l(3, b), close4]
            LINKS = [2 * 11, 2 * 8, 2 * 8, 2 * 12, 2 * 7]
            for p in range(5):
                def step(mb, eb):
                    if mb and p == 0:
                        sums(mb)
                    if eb:
                        close[p](eb)
                        operand(p, eb)
                q.sweep(step, LINKS[p])
                if p == 1:
                    dve.wait_ge(s_neg, 2 * B)
                    dve.tensor_reduce(negtot, negsum, AXX, ALU.add).then_inc(s_nt, 1)
                    dve.wait_ge(s_na, 1)
                    dve.tensor_scalar(flag, negall, 0.0, None, ALU.is_gt).then_inc(s_flag, 1)

            dve.wait_ge(s_d2, 5 * B)
            tmp = region_m[:, 0:T * V].rearrange("p (t v) -> p t v", v=V)

            def three_parts(src, parts):
                for k in range(3):
                    link(dve.tensor_copy(parts(k), src))
                    if k < 2:
                        link(dve.tensor_tensor(src, src, parts(k), ALU.subtract))
            dve.wait_ge(s_cc, 5 * B)
            three_parts(uraw, lambda k: upos[:, :, k * V:(k + 1) * V])
            for k in range(3):
                for a in range(2):
                    st = dve.tensor_copy(uneg[:, :, k * V + a * HEADS:k * V + (a + 1) * HEADS],
                                         upos[:, :, k * V + (1 - a) * HEADS:k * V + (2 - a) * HEADS])
            st.then_inc(s_u, 1)

            def masks5(blk, h):
                dve.wait_ge(arrived[slot(5, blk)][h], uses(5, blk))
                wait(dve, s_s5, blk.at(2, h - 1))
                src = ring[:, slot(5, blk), h * HALF:(h + 1) * HALF, :]
                dve.tensor_scalar(mask5[:, h, 0], src, 0.0, None, ALU.is_gt)
                dve.tensor_scalar(mask5[:, h, 1], src, 0.0, None, ALU.is_lt).then_inc(s_m5, 1)

            def read_logits(blk):
                dve.wait_ge(s_s5, blk.at(2, 2))
                link(dve.tensor_reduce(small_e, ST[:, 0:IT * 3 * V].rearrange("p (i k v) -> p i v k", i=IT, k=3),
                                       AXX, ALU.add))
                dve.scalar_tensor_tensor(out=rows(e_f, blk), in0=small_e, scalar=ALPHA, in1=small_e,
                                         op0=ALU.mult, op1=ALU.max).then_inc(s_e5, 1)

            def gru_rows_(n, blk, E=E):
                dve.wait_ge(s_sig, n(1))
                for i in range(IT):
                    st = dve.tensor_tensor(two(gt)[:, i, :], E[i][:, 3 * D:4 * D], gates[:, i, 0:D], ALU.mult)
                link(st)
                for i in range(IT):
                    st = dve.tensor_tensor(two(gt)[:, i, :], E[i][:, 2 * D:3 * D], two(gt)[:, i, :], ALU.add)
                st.then_inc(s_th, 1)
                dve.wait_ge(s_tn, n(1))
                link(dve.tensor_tensor(two(gt), rows(X, blk), two(gn), ALU.subtract))
                link(dve.tensor_tensor(two(gt), two(gt), gates[:, :, D:2 * D], ALU.mult))

            def step5(mb, eb):
                if mb:
                    masks5(mb, 0)
                if eb:
                    read_logits(eb)
                if mb:
                    masks5(mb, 1)
                if eb:
                    gru_rows_(lambda k: eb.at(1, k), eb, [E[:, i, :] for i in range(IT)])
                    dve.tensor_tensor(rows(res_eo, eb), two(gt), two(gn), ALU.add).then_inc(s_go, 1)
            q.sweep(step5, 2 * 4)

            dve.wait_ge(s_e5, B)
            dve.wait_ge(s_s5, 2 * B)
            link(dve.tensor_scalar(tmp, e_f[:, :, :], LOG2E, NMAX, ALU.mult, ALU.min))
            link(dve.tensor_scalar(tmp, tmp, -NMAX, ROUND, ALU.max, ALU.add))
            link(dve.tensor_scalar(tmp, tmp, -ROUND, None, ALU.add))
            link(dve.scalar_tensor_tensor(out=nbits[:, :, :], in0=tmp, scalar=-LN2_HI, in1=e_f[:, :, :],
                                          op0=ALU.mult, op1=ALU.add))
            dve.scalar_tensor_tensor(out=nbits[:, :, :], in0=tmp, scalar=-LN2_LO, in1=nbits[:, :, :],
                                     op0=ALU.mult, op1=ALU.add).then_inc(s_ex, 1)
            dve.wait_ge(s_f, 1)
            link(dve.tensor_scalar(nneg[:, :, :], tmp, 1.0 / STEP, 7.5 / STEP, ALU.mult, ALU.add))
            link(dve.tensor_scalar(nneg[:, :, :], nneg[:, :, :], ROUND, None, ALU.add))
            link(dve.tensor_scalar(nneg[:, :, :], nneg[:, :, :], -ROUND, None, ALU.add))
            dve.tensor_scalar(nneg[:, :, :], nneg[:, :, :], -1.0, -float(MSHIFT), ALU.mult, ALU.add)
            link(dve.tensor_scalar(nbits[:, :, :], tmp, 128.0, None, ALU.mult))
            link(dve.tensor_copy(tmp, e_f[:, :, :]))
            three_parts(tmp, lambda k: fpart[:, :, :, k])
            rpos = region_m[:, 512:512 + T * HEADS].rearrange("p (t h) -> p t h", h=HEADS)
            link(dve.reciprocal(rpos, e_f[:, :, 0:HEADS]))
            for h in range(HEADS):
                hw = HW[:, :, h * D:(h + 1) * D]
                st = dve.tensor_tensor(hw, hw, e_f[:, :, h:h + 1].broadcast_to([P, T, D]), ALU.mult)
            dve.tensor_tensor(e_f[:, :, HEADS:V], e_f[:, :, HEADS:V], rpos, ALU.mult).then_inc(s_fp, 1)
            dve.wait_ge(s_fp, 1)

            dve.wait_ge(s_go, B + 1)
            dve.wait_ge(s_eos, 16)
            any_negative = dve.value_load(flag[0:1, 0:1], min_val=0, max_val=1)

            def mask(blk, half):
                dve.wait_ge(arrived[slot(6, blk)][half], uses(6, blk))
                tiles = slice(half * HALF, (half + 1) * HALF)
                dve.tensor_scalar(mask6[:, blk.c % 2, tiles, :], ring[:, slot(6, blk), tiles, :], 0.0, -1.0,
                                  ALU.is_gt, ALU.mult).then_inc(s_mk, 1)

            def maximum(blk, c):
                half, h = divmod(c, HEADS)
                k = cand[:, c % 2]
                if c in ACT_CHUNKS:
                    dve.wait_ge(s_cd, blk.at(len(ACT_CHUNKS), 1 + ACT_CHUNKS.index(c)))
                else:
                    dve.wait_ge(s_mk, blk.at(2, half + 1))
                    for t in range(HALF):
                        tt = half * HALF + t
                        st = dve.tensor_scalar(k[:, t, :], mask6[:, blk.c % 2, tt, :], nneg[:, tt, h:h + 1], None,
                                               ALU.mult)
                    link(st)
                link(dve.tensor_tensor(k[:, 0:6, :], k[:, 0:6, :], k[:, 6:12, :], ALU.max))
                link(dve.tensor_tensor(k[:, 0:3, :], k[:, 0:3, :], k[:, 3:6, :], ALU.max))
                dve.tensor_tensor(k[:, 0, :], k[:, 0, :], k[:, 1, :], ALU.max)
                link(dve.tensor_tensor(k[:, 2, :], k[:, 2, :], k[:, 12, :], ALU.max))
                if half == 0:
                    if blk.c:
                        dve.wait_ge(s_par, blk.at(HEADS, h + 1 - HEADS))
                    dve.tensor_tensor(kmax[:, h, :], k[:, 0, :], k[:, 2, :], ALU.max).then_inc(s_tree, 1)
                else:
                    dve.tensor_tensor(k[:, 0, :], k[:, 0, :], k[:, 2, :], ALU.max).then_inc(s_tree, 1)
                    dve.wait_ge(s_tree, blk.at(V, c + 1))
                    dve.tensor_tensor(kmax[:, h, :], kmax[:, h, :], k[:, 0, :], ALU.max).then_inc(s_mx, 1)

            def weigh(blk, c):
                half, h = divmod(c, HEADS)
                tiles = slice(half * HALF, (half + 1) * HALF)
                dve.wait_ge(s_t, blk.at(V, c + 1))
                dve.tensor_tensor(pow_i[:, c % 2], pow_i[:, c % 2], mask6[:, blk.c % 2, tiles, :],
                                  ALU.bitwise_and).then_inc(s_tm, 1)
                dve.wait_ge(s_tm, blk.at(V, c + 1))
                dve.tensor_tensor(weight[:, c % 2], ring[:, slot(6, blk), tiles, :], pow_b[:, c % 2], ALU.mult)\
                    .then_inc(s_w, 1)

            def neg_maxima(blk):
                dve.wait_ge(arrived[slot(6, blk)][1], uses(6, blk))
                dve.wait_ge(s_tree, blk.at(V, HEADS))
                n = 0
                for t in range(T):
                    for h in range(HEADS):
                        v = HEADS + h
                        for ins in (lambda: dve.tensor_scalar(kneg, ring[:, slot(6, blk), t, :], 0.0,
                                                              nneg[:, t, v:v + 1], ALU.is_lt, ALU.mult),
                                    lambda: dve.tensor_scalar(kneg, kneg, -1.0, None, ALU.mult),
                                    lambda: dve.tensor_tensor(kmax[:, h, :], kmax[:, h, :], kneg, ALU.max)):
                            n += 1
                            ins().then_inc(s_q2, 1)
                            dve.wait_ge(s_q2, blk.at(NEG_LINKS, n))
                assert n == NEG_LINKS

            def neg_weigh(blk, half):
                dve.wait_ge(s_c6, blk.at(V, (half + 1) * HEADS))
                tiles = slice(half * HALF, (half + 1) * HALF)
                a = ring[:, slot(6, blk), tiles, :]
                for h in range(HEADS):
                    k = half * HEADS + h + 1
                    dve.wait_ge(s_t2, blk.at(V, k))
                    dve.tensor_scalar(pow_i[:, 0], pow_i[:, 0], 32512.0, None, ALU.min).then_inc(s_q3, 1)
                    dve.wait_ge(s_q3, blk.at(V, k))
                    dve.scalar_tensor_tensor(out=pow_b[:, 0], in0=a, scalar=0.0, in1=pow_b[:, 0],
                                             op0=ALU.is_lt, op1=ALU.mult).then_inc(s_tm2, 1)
                    dve.wait_ge(s_tm2, blk.at(V, k))
                    for t in range(HALF):
                        tt = half * HALF + t
                        st = dve.scalar_tensor_tensor(out=weight[:, 0, t, :], in0=a[:, t, :],
                                                      scalar=e_f[:, tt, HEADS + h:HEADS + h + 1],
                                                      in1=pow_b[:, 0, t, :], op0=ALU.mult, op1=ALU.mult)
                    st.then_inc(s_w2, 1)
                    dve.wait_ge(s_c2, blk.at(V, k))

            def sum_heads(blk):
                dve.wait_ge(s_tr, blk.at(1, 1))
                link(dve.tensor_reduce(zz, DEN[blk.c % 2][:, 0:IT * 9]
                                       .rearrange("p (i h k) -> p i h k", i=IT, h=HEADS),
                                       AXX, ALU.add))
                link(dve.tensor_scalar(zz, zz, TINY, float(HEADS), ALU.max, ALU.mult))
                link(dve.reciprocal(rz, zz))
                for h in range(HEADS):
                    for i in range(IT):
                        dst = xt_es[:, bass.ds(blk.at(W, i * D), D)]
                        src = two(hsum[h])[:, i, :]
                        if h == 0:
                            st = dve.tensor_scalar(dst, src, rz[:, i, h:h + 1], None, ALU.mult)
                        else:
                            st = dve.scalar_tensor_tensor(out=dst, in0=src, scalar=rz[:, i, h:h + 1], in1=dst,
                                                          op0=ALU.mult, op1=ALU.add)
                    if h < HEADS - 1:
                        link(st)
                st.then_inc(s_es, 1)

            def step6(xb, wb, sb_):
                for c in range(V):
                    half, h = divmod(c, HEADS)
                    if xb and h == 0:
                        mask(xb, half)
                    if xb and c == HEADS:
                        with dve.If(any_negative):
                            neg_maxima(xb)
                            alone(dve)
                    if wb:
                        weigh(wb, c)
                    if xb:
                        maximum(xb, c)
                    if sb_ and c == 3:
                        sum_heads(sb_)
                    if wb and h == HEADS - 1:
                        with dve.If(any_negative):
                            neg_weigh(wb, half)
                            alone(dve)
                        dve.wait_ge(s_dve, wb.at(2, 2 * B + half))
                        alone(dve)
                        dve.memset(cell, 0.0).then_inc(s_dve, 1)
            q.sweep_three(step6, 2 * (V * 3 + V - len(ACT_CHUNKS) + 5))

            dve.wait_ge(s_n, 48)

            def step7(_, blk):
                if not blk:
                    return
                gru_rows_(lambda k: blk.at(1, B + k), blk,
                          [E[:, i, :] for i in range(IT)] if blk.c % 2 == 0 else GATE[1])
                dve.tensor_tensor(two(gt), two(gt), two(gn), ALU.add).then_inc(s_go, 1)
                dve.wait_ge(s_go, g(1, blk, 1, 2))
                link(dve.tensor_tensor(two(gt), two(gt), rows(eo7, blk), ALU.add))
                for i in range(IT):
                    xi = X[:, bass.ds(blk.at(IT, i), 1), :].rearrange("p i f -> p (i f)")
                    st = dve.scalar_tensor_tensor(out=xi, in0=two(gt)[:, i, :], scalar=col(dg, blk, i), in1=xi,
                                                  op0=ALU.mult, op1=ALU.add)
                link(st)
                alone(dve)
                for i in range(IT):
                    xi = X[:, bass.ds(blk.at(IT, i), 1), :].rearrange("p i f -> p (i f)")
                    st = dve.bn_stats(bs[:, i, :], xi)
                link(st)
                alone(dve)
                for i in range(IT):
                    st = dve.bn_aggr(mv[:, i, :], bs[:, i, :])
                link(st)
                alone(dve)
                link(dve.tensor_copy(rows(norm, blk), mv))
            q.sweep(step7, 2 * 8)
            dve.tensor_copy(e_f[:, :, 0], norm[:, :, 0]).then_inc(s_var, 1)
            dve.wait_ge(s_std, vbase[5] + 1)
            link(dve.reciprocal(e_f[:, :, 1], norm[:, :, 0]))
            for t in range(T):
                st = dve.tensor_scalar(res_eo[:, t, :], X[:, t, :], e_f[:, t, 0:1], e_f[:, t, 1:2],
                                       ALU.subtract, ALU.mult)
            st.then_inc(s_fin, 1)


def kernel(x, adj, L0_gnn_W, L1_gnn_W1, L1_gnn_b1, L1_gnn_W2, L1_gnn_b2, L1_gnn_W3, L1_gnn_b3,
           L1_gnn_g1, L1_gnn_be1, L1_gnn_g2, L1_gnn_be2, L1_gnn_g3, L1_gnn_be3,
           L2_gnn_weight, L2_gnn_bias, L3_gnn_gat_W, L3_gnn_gat_a,
           L3_gnn_edge_Wih, L3_gnn_edge_Whh, L3_gnn_edge_bih, L3_gnn_edge_bhh,
           L3_gnn_node_Wih, L3_gnn_node_Whh, L3_gnn_node_bih, L3_gnn_node_bhh):
    import numpy as np
    import concourse.bacc as bacc
    from concourse.bass_utils import run_bass_kernel_spmd

    def arr(a):
        return np.asarray(a)

    x, adj = arr(x), arr(adj)
    NP_ = T * P
    off = np.zeros((NP_, NP_), np.float32)
    off[:N, :N] = adj.T
    node = np.arange(NP_)
    off[node, node] = 0.0
    dgn = np.ones(NP_, np.float32)
    dgn[:N] = adj[np.arange(N), np.arange(N)]
    xp = np.zeros((NP_, D), np.float32)
    xp[:N] = x
    a = arr(L3_gnn_gat_a)[:, :, 0].reshape(HEADS, 2, D)
    gw = arr(L3_gnn_gat_W)

    def wide(v):
        return np.broadcast_to(arr(v), (P, D))
    w0 = arr(L0_gnn_W)
    consts = np.concatenate(
        [w0[:, :D].T, w0[:, D:].T, arr(L1_gnn_W1), arr(L1_gnn_W2), arr(L1_gnn_W3), arr(L2_gnn_weight),
         gw.transpose(1, 0, 2).reshape(D, -1), gw.transpose(2, 0, 1).reshape(D, -1),
         a.transpose(2, 0, 1).reshape(D, V)]
        + [wide(v) for v in (L1_gnn_g1, L1_gnn_be1, L1_gnn_g2, L1_gnn_be2, L1_gnn_g3, L1_gnn_be3, L2_gnn_bias)],
        axis=1)
    rows = np.concatenate([arr(v) for v in (L1_gnn_b1, L1_gnn_b2, L1_gnn_b3, L3_gnn_edge_bih, L3_gnn_edge_bhh)])
    arrays = {
        "adjt": off.reshape(T, P, B, W).transpose(2, 1, 0, 3),
        "diag": dgn.reshape(T, P).T,
        "xrow": xp.reshape(T, P, D).transpose(1, 0, 2).reshape(P, T * D),
        "xcol": xp.T,
        "consts": consts,
        "rows": rows[None],
        "gru": np.stack([np.concatenate([arr(i).T, arr(h).T], axis=1) for i, h in
                         ((L3_gnn_edge_Wih, L3_gnn_edge_Whh), (L3_gnn_node_Wih, L3_gnn_node_Whh))]),
        "gru_rows": np.concatenate([arr(L3_gnn_node_bih), arr(L3_gnn_node_bhh)])[None],
        "ident": np.eye(P, dtype=np.float32),
    }
    arrays = {k: np.ascontiguousarray(v) for k, v in arrays.items()}
    nc = bacc.Bacc("TRN2", target_bir_lowering=False, num_devices=1)
    args = {k: nc.dram_tensor(k + "_dram", v.shape, F32, kind="ExternalInput").ap() for k, v in arrays.items()}
    out = nc.dram_tensor("out_dram", (NP_, D), F32, kind="ExternalOutput").ap()
    edge_gru = nc.dram_tensor("edge_gru_dram", (P, T, D), F32, kind="Internal").ap()
    build(nc, edge_gru=edge_gru, out=out, **args)
    r = run_bass_kernel_spmd(nc, [{k + "_dram": v for k, v in arrays.items()}], core_ids=[0])
    return r.results[0]["out_dram"][:N]
```

```python
from contextlib import ExitStack

import concourse.bass as bass
from concourse import mybir

ALU = mybir.AluOpType
ACT = mybir.ActivationFunctionType
F32 = mybir.dt.float32
BF16 = mybir.dt.bfloat16
I16 = mybir.dt.int16
AXX = mybir.AxisListType.X

N = 3327
P = 128
D = 128
T = -(-N // P)
W = 256
B = T * P // W
IT = W // P
HALF = T // 2
HEADS = 3
V = 2 * HEADS
EPS = 1e-5
ALPHA = 0.2
LOG2E = 1.4426950408889634
LN2_HI = 0.693359375
LN2_LO = -2.12194440e-4
ROUND = 12582912.0
STEP = 16
MSHIFT = 2 ** 14
NMAX = float(STEP * (MSHIFT - 1))
TINY = 1e-30

C_WAB, C_W1, C_W4, C_GW, C_GWT, C_GA = 0, 256, 640, 768, 1152, 1536
C_GB = C_GA + 6
C_END = C_GB + 7 * D
BK = 6
R_B, R_END = 0, 3 * D
R_GRU = 8 * D


class Block:

    def __init__(self, c, r=0):
        self.c, self.r = c, r

    def at(self, k, base=0):
        return self.r * (2 * k) + (base + k * self.c)

    def cols(self, k):
        return bass.ds(self.at(k), k)


def sweep(eng, step):
    step(Block(0), None)
    with eng.Fori(0, (B - 1) // 2) as r:
        step(Block(1, r), Block(0, r))
        step(Block(2, r), Block(1, r))
    step(None, Block(B - 1))


def sweep_three(eng, step, turn=lambda r: None):
    step(Block(0), None, None)
    step(Block(1), Block(0), None)
    with eng.Fori(0, (B - 3) // 2) as r:
        turn(r)
        step(Block(2, r), Block(1, r), Block(0, r))
        step(Block(3, r), Block(2, r), Block(1, r))
    turn(0)
    step(Block(B - 1), Block(B - 2), Block(B - 3))
    step(None, Block(B - 1), Block(B - 2))
    step(None, None, Block(B - 1))


def build(nc, adjt, diag, xrow, xcol, consts, rows, gru, gru_rows, ident, zt, out):
    ctx = ExitStack()
    with ctx:
        def sb(name, shape, dt=F32):
            return ctx.enter_context(nc.sbuf_tensor(name, shape, dt))

        def sem(name):
            return ctx.enter_context(nc.semaphore(name))

        ring = sb("ring", [P, 2, T, W])
        X = sb("X", [P, T, D])
        res = sb("res", [P, T, D])
        xt_es = sb("xt_es", [P, T * D])
        FW = sb("FW", [P, 2, T * D])
        HW = sb("HW", [P, T, HEADS * D])
        region_m = sb("region_m", [P, T * W])
        region_t = sb("region_t", [P, T * D])
        stage = sb("stage", [P, 2048])
        zbuf = sb("zbuf", [P, W])
        idn = sb("idn", [P, P])
        dg = sb("dg", [P, T])
        small = sb("small", [P, 80])
        e_f = sb("e_f", [P, T, V])
        nbits = sb("nbits", [P, T, V])
        nneg = sb("nneg", [P, T, V])
        fpart = sb("fpart", [P, T, V, 3], BF16)

        cst = region_m[:, 0:C_END]
        wab = cst[:, C_WAB:C_WAB + 2 * D]
        gat_w = cst[:, C_GW:C_GW + HEADS * D]
        gat_wt = cst[:, C_GWT:C_GWT + HEADS * D]
        gat_a = cst[:, C_GA:C_GA + V]
        wa = region_m[:, C_END:C_END + V]

        def gb(k):
            return cst[:, C_GB + k * D:C_GB + (k + 1) * D]

        brow = region_t[0:BK, 0:R_END // 2].bitcast(BF16)
        o = R_END // 2
        xts = region_t[:, o:o + W]
        colsum = region_t[:, o + W:o + 5 * W].rearrange("p (k h c) -> p k h c", k=2, h=2)
        o += 5 * W
        uraw = region_t[:, o:o + T * V].rearrange("p (t v) -> p t v", v=V)
        o += T * V
        upos = region_t[:, o:o + T * 9].bitcast(BF16).rearrange("p (t k) -> p t k", k=3 * V)
        o += T * 9
        uneg = region_t[:, o:o + T * 9].bitcast(BF16).rearrange("p (t k) -> p t k", k=3 * V)
        o += T * 9
        norm = region_t[:, o:o + T * 2].rearrange("p (t k) -> p t k", k=2)
        o += T * 2
        ones = region_t[0:BK, o:o + P // 2].bitcast(BF16)
        assert o + P // 2 <= T * D

        mask5 = region_m[:, :].bitcast(BF16).rearrange("p (h s t c) -> p h s t c", h=2, s=2, t=HALF)
        mask6 = region_m[:, :].bitcast(I16).rearrange("p (k t c) -> p k t c", k=2, t=T)
        cand = res[:, :, :].rearrange("p t f -> p (t f)").bitcast(I16)\
            .rearrange("p (k t c) -> p k t c", k=2, t=HALF)
        hw_flat = HW[:, :, :].rearrange("p t f -> p (t f)")
        dump = hw_flat[:, 0:HALF * W].rearrange("p (t c) -> p t c", t=HALF)
        split = [hw_flat[0:BK, 0:3 + R_END], hw_flat[0:BK, R_END + 8:R_END + 8 + R_END // 2].bitcast(BF16)]
        res_flat = res[:, :, :].rearrange("p t f -> p (t f)")
        split7 = [res_flat[0:BK, 0:3 + R_GRU], res_flat[0:BK, R_GRU + 8:R_GRU + 8 + R_GRU // 2].bitcast(BF16)]
        gru_w = res_flat[:, (T - 12) * D:].rearrange("p (k s f) -> p k s f", k=2, s=2)
        assert R_GRU + 8 + R_GRU // 2 <= (T - 12) * D
        z7 = region_m[:, 0:B * W]
        pow_i = region_t[:, :].bitcast(I16).rearrange("p (k t c) -> p k t c", k=2, t=HALF)
        pow_b = region_t[:, :].bitcast(BF16).rearrange("p (k t c) -> p k t c", k=2, t=HALF)
        weight = FW[:, :, :].rearrange("p k (t c) -> p k t c", t=HALF)

        def stg(k):
            return stage[:, k * W:(k + 1) * W]
        xs, zs, xTs, ys = (stg(k) for k in range(4))

        def more(k, n=1):
            return region_m[:, (B + k) * W:(B + k + n) * W]
        gates = [g_.rearrange("p (i c) -> p i c", i=IT) for g_ in (stage[:, 4 * W:6 * W], more(0, 2))]
        gn, gt = [stg(6), more(2)], [stg(7), more(3)]
        edge_rows = more(4)
        brow7 = more(10, 2)[0:BK, :].bitcast(BF16)
        ones7 = more(12)[0:BK, 0:P // 2].bitcast(BF16)
        stats = more(9)[:, 0:T * 2].rearrange("p (t k) -> p t k", k=2)
        h7, x7 = [xTs, more(5)], [[more(6), more(7)], [zs, more(8)]]
        kmax = stage[:, 0:3 * W // 2].bitcast(I16).rearrange("p (h c) -> p h c", h=HEADS)
        kneg = stage[:, 3 * W // 2:2 * W].bitcast(I16)
        negk = stage[:, 2 * W:5 * W].rearrange("p (h c) -> p h c", h=HEADS)
        heads_t = stage[:, 5 * W:8 * W].rearrange("p (h c) -> p h c", h=HEADS)

        def two(ap):
            return ap.rearrange("p (i f) -> p i f", i=IT)

        sd = small[:, 0:4].rearrange("p (i k) -> p i k", i=IT)
        rec = small[:, 4:6]
        drec = small[:, 6:8]
        bs = small[:, 8:20].rearrange("p (i k) -> p i k", i=IT)
        mv = small[:, 20:24].rearrange("p (i k) -> p i k", i=IT)
        std = small[:, 24:28]
        rstd = small[:, 28:30]
        eps = small[:, 30:31]
        one = small[:, 77:78]
        diag1 = small[:, 31:33]
        zz = small[:, 33:39].rearrange("p (i h) -> p i h", i=IT)
        rz = small[:, 39:45].rearrange("p (i h) -> p i h", i=IT)
        small_e = small[:, 33:45].rearrange("p (i v) -> p i v", i=IT)
        cell = small[:, 45:46]
        negsum = small[:, 48:48 + T]
        negtot, negall = small[:, 74:75], small[:, 75:76]
        flag = small[:, 76:77].bitcast(mybir.dt.int32)

        def ps(name, banks=1):
            return ctx.enter_context(nc.psum_tensor(name, [P, 512 * banks], F32))
        ZP = ps("Z", 2).rearrange("p (i c) -> p i c", i=IT)
        Z = [ZP[:, 0, :], ZP[:, 1, :]]
        TP, HB, HC, ST = ps("TP"), ps("HB"), ps("HC"), ps("ST")
        E = ps("E", 2).rearrange("p (i c) -> p i c", i=IT)
        NUMB = [(Z[0], Z[1]), (E[:, 0, :], E[:, 1, :])]
        tp, hb, hc = (x[:, 0:W] for x in (TP, HB, HC))
        DEN = [ST, TP]
        hsum = [hb, HB[:, W:2 * W], hc]
        GATE = [E, ZP]

        s_c = sem("constants_in")
        s_x = sem("x_in")
        s_xc = sem("x_transposed_in")
        s_n = sem("gru_weights_in")
        s_z7 = [sem("neighbour_sums_in"), sem("last_neighbour_sum_in")]
        s_nr = sem("gru_rows_split")
        arrived = [[sem(f"arrived_{s}{h}") for h in range(2)] for s in range(2)]
        s_init = sem("init_done")
        s_pe = sem("pe_half_done")
        s_dve = sem("dve_half_done")
        s_wa = sem("wa_product")
        s_was = sem("wa_stored")
        s_zs = sem("zs_ready")
        s_a = sem("closing_a_done")
        s_var = sem("to_sqrt")
        s_std = sem("sqrt_done")
        s_d1 = sem("rows_ready")
        s_b = sem("rows_transposed")
        s_xt = sem("xTs_ready")
        s_cc = sem("closing_c_done")
        s_d2 = sem("operand_ready")
        s_u = sem("u_parts_ready")
        s_m5 = sem("sign_masks_ready")
        s_s5 = sem("logits_half_done")
        s_e5 = sem("logits_read")
        s_sig = sem("gates_done")
        s_th = sem("to_tanh")
        s_tn = sem("tanh_done")
        s_go = sem("gru_done")
        s_ex = sem("to_exp")
        s_f = sem("exp_done")
        s_fp = sem("f_parts_ready")
        s_hw = sem("hw_scaled")
        s_neg = sem("negatives_summed")
        s_nt = sem("negatives_total")
        s_na = sem("negatives_reduced")
        s_flag = sem("flag_ready")
        s_zo = sem("neighbour_sum_out")
        s_mk = sem("mask_half_ready")
        s_cd = sem("candidates_ready")
        s_tree = sem("candidates_reduced")
        s_mx = sem("max_ready")
        s_par = sem("max_reduced")
        s_nk = sem("negk_ready")
        s_t = sem("powers_ready")
        s_tm = sem("powers_masked")
        s_w = sem("weights_ready")
        s_z6 = sem("powers_multiplied")
        s_c6 = sem("chunk_done")
        s_t2 = sem("neg_powers_ready")
        s_tm2 = sem("neg_powers_masked")
        s_w2 = sem("neg_weights_ready")
        s_c2 = sem("neg_chunk_done")
        s_q2 = sem("dve_neg_chain")
        s_q3 = sem("neg_powers_finite")
        s_ev = sem("heads_copied")
        s_tr = sem("heads_transposed")
        s_es = sem("heads_summed")
        s_q = sem("dve_chain")
        s_out = sem("out_written")
        s_fin = sem("final_rows")

        ACT_CHUNKS = (1, 2, 4, 5)
        ACT_FIRST = (1, 4)
        NEG_LINKS = T * HEADS * 3
        VAR = [2, 1, 1, 2, 1]
        vbase = [B * sum(VAR[:p]) for p in range(6)]

        def wait(eng, semaphore, value):
            if not (isinstance(value, int) and value <= 0):
                eng.wait_ge(semaphore, value)

        def alone(eng):
            eng.nop(nofuse=True)

        class Links:

            def __init__(self, eng, semaphore):
                self.eng, self.sem = eng, semaphore
                self.done, self.turn = 0, 0

            def mark(self, ins):
                ins.then_inc(self.sem, 1)
                self.done += 1

            def settle(self):
                self.eng.wait_ge(self.sem, self.turn + self.done)

            def link(self, ins):
                self.mark(ins)
                self.settle()

            def sweep(self, step, per):
                step(Block(0), None)
                before = self.done
                with self.eng.Fori(0, (B - 1) // 2) as r:
                    self.turn = r * per
                    step(Block(1, r), Block(0, r))
                    step(Block(2, r), Block(1, r))
                self.turn = 0
                assert self.done - before == per, (self.done - before, per)
                self.done = before + per * ((B - 1) // 2)
                step(None, Block(B - 1))

            def sweep_three(self, step, per):
                def turn(r):
                    if isinstance(r, int):
                        self.turn = 0
                        assert self.done - self.before == per, (self.done - self.before, per)
                        self.done = self.before + per * ((B - 3) // 2)
                    else:
                        self.before = self.done
                        self.turn = r * per
                sweep_three(self.eng, step, turn)

        def slot(p, blk):
            return (p * B + blk.c) % 2

        def uses(p, blk, k=0):
            return blk.r * 16 + 16 * ((p * B + blk.c) // 2 + 1)

        def g(p, blk, k, more=0):
            return blk.at(k, k * p * B + more)

        block = ctx.enter_context(nc.Block())

        @block.sync
        def _(sp):
            sp.dma_start(FW[:, 0, :], xrow).then_inc(s_x, 16)

            def load_constants():
                sp.dma_start(split[0], rows).then_inc(s_c, 16)
                sp.dma_start(cst, consts).then_inc(s_c, 16)
                sp.dma_start(dg[:, :], diag).then_inc(s_c, 16)
                sp.dma_start(idn[:, :], ident).then_inc(s_c, 16)
                sp.dma_start(xt_es[:, :], xcol).then_inc(s_xc, 16)

            def load(p, blk, pe_wait=None, dve_wait=None):
                for h in range(2):
                    if pe_wait is not None:
                        sp.wait_ge(s_pe, pe_wait(h))
                    if dve_wait is not None:
                        alone(sp)
                        sp.wait_ge(*dve_wait(h))
                    src = adjt[bass.ds(blk.at(1), 1), :, h * HALF:(h + 1) * HALF, :]
                    sp.dma_start(ring[:, slot(p, blk), h * HALF:(h + 1) * HALF, :],
                                 src.rearrange("a p t c -> (a p) t c"))\
                        .then_inc(arrived[slot(p, blk)][h], 16)

            DB = {0: (s_dve, 0), 1: (s_neg, 0), 5: (s_m5, 0), 6: (s_dve, 2 * B)}
            for p in range(7):
                def pe_wait(blk):
                    if p == 5:
                        return None
                    return lambda h: g(min(p, 5), blk, 2, h - 3)

                def dve_wait(blk):
                    if p not in DB:
                        return None
                    return lambda h: (DB[p][0], blk.at(2, DB[p][1] + h - 3))

                for c in range(2):
                    if p == 0:
                        load(p, Block(c))
                        if c == 0:
                            load_constants()
                    elif p == 6:
                        load(p, Block(c), None, lambda h: (s_m5, 2 * (B - 2 + c) + h + 1))
                    elif p == 5:
                        load(p, Block(c), lambda h: g(5, Block(c), 2, h - 3))
                    else:
                        load(p, Block(c), pe_wait(Block(c)),
                             {1: lambda h: (s_dve, 2 * (B - 2 + c) + h + 1),
                              2: lambda h: (s_neg, 2 * (B - 2 + c) + h + 1)}.get(p))
                with sp.Fori(0, (B - 3) // 2) as r:
                    load(p, Block(2, r), pe_wait(Block(2, r)), dve_wait(Block(2, r)))
                    load(p, Block(3, r), pe_wait(Block(3, r)), dve_wait(Block(3, r)))
                last = Block(B - 1)
                load(p, last, pe_wait(last), dve_wait(last))
            sp.wait_ge(s_mx, HEADS * B)
            sp.dma_start(split7[0], gru_rows).then_inc(s_n, 16)
            sp.dma_start(gru_w, gru).then_inc(s_n, 16)
            sp.wait_ge(s_dve, 4 * B)
            sp.wait_ge(s_zo, 16 * (B - 1) + 1)
            sp.dma_start(z7[:, 0:(B - 1) * W].rearrange("p (b c) -> p b c", b=B - 1),
                         zt[0:B - 1].rearrange("b p c -> p b c")).then_inc(s_z7[0], 16)
            sp.wait_ge(s_zo, 16 * B + 1)
            sp.dma_start(z7[:, (B - 1) * W:B * W], zt[B - 1]).then_inc(s_z7[1], 16)
            for h in range(2):
                sp.wait_ge(s_fin, h + 1)
                tiles = slice(h * HALF, (h + 1) * HALF)
                sp.dma_start(out.rearrange("(t p) f -> p t f", p=P)[:, tiles, :], res[:, tiles, :])\
                    .then_inc(s_out, 16)
            sp.wait_ge(s_out, 32)

        @block.tensor
        def _(pe):
            pe.wait_ge(s_x, 16)

            def main(p, blk, t0, t1):
                zz_ = NUMB[blk.c % 2][1][:, W:2 * W] if p == 6 else Z[slot(p, blk)][:, 0:W]
                for t in range(t0, t1):
                    if t in (0, HALF):
                        pe.wait_ge(arrived[slot(p, blk)][t // HALF], uses(p, blk))
                    f = X[:, t, :] if p == 6 else FW[:, p % 2, t * D:(t + 1) * D]
                    mm = pe.matmul(zz_, f, ring[:, slot(p, blk), t, :], start=t == 0, stop=t == T - 1,
                                   skip_group_check=p == 6)
                    if t in (HALF - 1, T - 1):
                        mm.then_inc(s_pe, 1)

            def step_a(p, blk):
                pe.wait_ge(s_zs, g(p, blk, 1, 1))
                if p == 0:
                    pe.wait_ge(s_dve, blk.at(2, 2))
                    for i in range(IT):
                        s = slice(i * P, (i + 1) * P)
                        pe.matmul(E[:, i, 0:2 * D], xts[:, s], wab, start=True, stop=True)
                        pe.matmul(E[:, i, 2 * D:3 * D], zs[:, s], wab[:, D:2 * D], start=True, stop=True)
                        pe.matmul(E[:, i, 3 * D:3 * D + 1], colsum[:, blk.c % 2, 0, s], one, start=True, stop=False)
                        last = pe.matmul(E[:, i, 3 * D:3 * D + 1], colsum[:, blk.c % 2, 1, s], one,
                                         start=False, stop=True)
                    last.then_inc(s_a, 1)
                else:
                    for i in range(IT):
                        last = pe.transpose(two(tp)[:, i, :], zs[:, i * P:(i + 1) * P], idn[:, :])
                    last.then_inc(s_a, 1)

            def step_b(p, blk):
                pe.wait_ge(s_d1, g(p, blk, 1, 1))
                for i in range(IT):
                    last = pe.transpose(two(hb)[:, i, :], xs[:, i * P:(i + 1) * P], idn[:, :])
                last.then_inc(s_b, 1)

            def step_c(p, blk):
                if p == 3:
                    wgt = cst[:, C_W4:C_W4 + D]
                elif p < 3:
                    wgt = cst[:, C_W1 + p * D:C_W1 + (p + 1) * D]
                pe.wait_ge(s_xt, g(p, blk, 1, 1))
                alone(pe)
                pe.wait_ge(s_d2, g(p, blk, 1, 1))
                for i in range(IT):
                    lhs = xTs[:, i * P:(i + 1) * P]
                    if p == 4:
                        pe.matmul(E[:, i, 0:3 * D], lhs, gat_w, start=True, stop=True)
                        last = pe.matmul(E[:, i, 3 * D:3 * D + V], lhs, wa, start=True, stop=True)
                    else:
                        if p < 3:
                            pe.matmul(two(hc)[:, i, :], ones, brow[:, R_B + p * D:R_B + (p + 1) * D],
                                      start=i == 0, stop=False, skip_group_check=True)
                        last = pe.matmul(two(hc)[:, i, :], lhs, wgt, start=p == 3 and i == 0, stop=True,
                                         skip_group_check=True)
                last.then_inc(s_cc, 1)

            def step(p, mb, eb, cb):
                main(p, mb, 0, 3)
                if eb:
                    step_a(p, eb)
                if cb:
                    step_c(p, cb)
                main(p, mb, 3, 23)
                if eb:
                    step_b(p, eb)
                main(p, mb, 23, T)

            def seam(p):
                mb, eb, cb = Block(0), Block(B - 1), Block(B - 2)
                if p == 4:
                    step_a(p, eb)
                    step_c(p, cb)
                    step_b(p, eb)
                    step_c(p, eb)
                    return
                pe.wait_ge(s_d2, p * B + B - 1)
                main(p + 1, mb, 0, 3)
                step_a(p, eb)
                step_c(p, cb)
                main(p + 1, mb, 3, T - 2 * IT)
                step_b(p, eb)
                pe.wait_ge(s_d2, (p + 1) * B)
                main(p + 1, mb, T - 2 * IT, T - IT)
                step_c(p, eb)
                pe.wait_ge(s_d2, (p + 1) * B + 1)
                main(p + 1, mb, T - IT, T)

            main(0, Block(0), 0, T)
            pe.wait_ge(s_c, 64)
            pe.wait_ge(s_init, 5)
            for h in range(HEADS):
                last = pe.matmul(ST[:, 2 * h:2 * h + 2], gat_wt[:, h * D:(h + 1) * D],
                                 gat_a[:, 2 * h:2 * h + 2], start=True, stop=True)
            last.then_inc(s_wa, 1)
            pe.wait_ge(s_was, 1)
            for p in range(5):
                step(p, Block(1), Block(0), None)
                with pe.Fori(0, (B - 3) // 2) as r:
                    step(p, Block(2, r), Block(1, r), Block(0, r))
                    step(p, Block(3, r), Block(2, r), Block(1, r))
                step(p, Block(B - 1), Block(B - 2), Block(B - 3))
                seam(p)

            def logits(blk, h):
                pe.wait_ge(s_m5, blk.at(2, h + 1))
                if h == 0:
                    wait(pe, s_e5, blk.at(1))
                for t in range(HALF):
                    for i in range(IT):
                        for s, u in ((0, upos), (1, uneg)):
                            first = h == 0 and t == 0 and i == 0 and s == 0
                            last = pe.matmul(ST[:, i * 3 * V:(i + 1) * 3 * V],
                                             mask5[:, h, s, t, i * P:(i + 1) * P], u[:, h * HALF + t, :],
                                             start=first, stop=h == 1 and t == HALF - 1 and s == 1,
                                             skip_group_check=True)
                last.then_inc(s_s5, 1)

            def step5(mb, _):
                if mb:
                    logits(mb, 0)
                    logits(mb, 1)
            pe.wait_ge(s_u, 1)
            sweep(pe, step5)

            pe.wait_ge(s_fp, 1)
            pe.wait_ge(s_hw, HEADS)
            pe.wait_ge(s_zs, 5 * B)
            pe.wait_ge(s_flag, 1)
            any_negative = pe.value_load(flag[0:1, 0:1], min_val=0, max_val=1)

            def products(blk, half, v, buf, masked, weighed, first, powers_used=None,
                         between=None):
                par, h = blk.c % 2, v % HEADS
                pe.wait_ge(*masked)
                for t in range(HALF):
                    for i in range(IT):
                        k = i * 9 + h * 3
                        last = pe.matmul(DEN[par][:, k:k + 3], pow_b[:, buf, t, i * P:(i + 1) * P],
                                  fpart[:, half * HALF + t, v, :],
                                  start=first and h == 0 and t == 0 and i == 0,
                                  stop=half == 1 and t == HALF - 1, skip_group_check=True)
                if powers_used is not None:
                    last.then_inc(powers_used, 1)
                    between()
                pe.wait_ge(*weighed)
                for t in range(HALF):
                    last = pe.matmul(NUMB[par][h // 2][:, h % 2 * W:(h % 2 + 1) * W],
                                     HW[:, half * HALF + t, h * D:(h + 1) * D], weight[:, buf, t, :],
                                     start=first and h == 0 and t == 0,
                                     stop=half == 1 and t == HALF - 1, skip_group_check=True)
                return last

            Z_TILES = [0, 4, 8, HALF, HALF + 4, HALF + 8, T]

            def step6(_, wb, sb_):
                for c in range(V):
                    half, h = divmod(c, HEADS)
                    if wb:
                        if c == 0:
                            wait(pe, s_es, wb.at(1) if wb.c else 0)
                        products(wb, half, h, c % 2, (s_tm, wb.at(V, c + 1)), (s_w, wb.at(V, c + 1)), half == 0, s_z6,
                                 lambda: main(6, wb, *Z_TILES[c:c + 2]))\
                            .then_inc(s_c6, 1)
                        if c % HEADS == HEADS - 1:
                            with pe.If(any_negative):
                                for n in range(HEADS):
                                    k = wb.at(V, half * HEADS + n + 1)
                                    products(wb, half, HEADS + n, 0, (s_tm2, k), (s_w2, k), False)\
                                        .then_inc(s_c2, 1)
                    if sb_ and c == 1:
                        pe.wait_ge(s_ev, sb_.at(1, 1))
                        alone(pe)
                        pe.wait_ge(s_es, sb_.at(1, 1))
                        for n in range(HEADS):
                            for i in range(IT):
                                last = pe.transpose(two(hsum[n])[:, i, :], heads_t[:, n, i * P:(i + 1) * P],
                                                    idn[:, :])
                        last.then_inc(s_tr, 1)
            sweep_three(pe, step6)

            pe.wait_ge(s_n, 32)
            pe.wait_ge(s_es, B + 1)
            pe.wait_ge(s_nr, 2)

            def gru_products(k, par):
                wih, whh = gru_w[:, k, 0, :], gru_w[:, k, 1, :]
                for i in range(IT):
                    s = slice(i * P, (i + 1) * P)
                    bank = GATE[k][:, i, :]
                    pe.matmul(bank[:, 0:4 * D], ones7, brow7[:, k * 4 * D:(k + 1) * 4 * D],
                              start=True, stop=False, skip_group_check=True)
                    pe.matmul(bank[:, 0:3 * D], x7[k][par][:, s], wih, start=False, stop=False,
                              skip_group_check=True)
                    pe.matmul(bank[:, 0:2 * D], h7[par][:, s], whh[:, 0:2 * D], start=False, stop=True,
                              skip_group_check=True)
                    last = pe.matmul(bank[:, 3 * D:4 * D], h7[par][:, s], whh[:, 2 * D:3 * D],
                                     start=False, stop=True, skip_group_check=True)
                last.then_inc(s_cc, 1)

            def step7(xb, mb, _):
                if xb:
                    pe.wait_ge(s_d1, g(5, xb, 1, 1))
                    for i in range(IT):
                        pe.transpose(two(hb)[:, i, :], xs[:, i * P:(i + 1) * P], idn[:, :])
                    for i in range(IT):
                        last = pe.transpose(two(tp)[:, i, :], ys[:, i * P:(i + 1) * P], idn[:, :])
                    last.then_inc(s_b, 1)
                if mb:
                    pe.wait_ge(s_xt, g(5, mb, 1, 1))
                    for k in range(2):
                        alone(pe)
                        wait(pe, s_th, mb.at(2, k - 1))
                        gru_products(k, mb.c % 2)
            sweep_three(pe, step7)

        @block.scalar
        def _(act):
            act.wait_ge(s_xc, 16)
            act.wait_ge(s_init, 5)
            act.wait_ge(s_wa, 1)
            act.activation(wa.rearrange("p (k h) -> p h k", k=2),
                           ST[:, 0:V].rearrange("p (h k) -> p h k", k=2), ACT.Copy).then_inc(s_was, 1)

            def copy_z(p, blk):
                act.wait_ge(s_pe, g(p, blk, 2, 2))
                if p == 0:
                    act.activation(xts, xt_es[:, blk.cols(W)], ACT.Copy)
                act.activation(zs, Z[slot(p, blk)][:, 0:W], ACT.Copy).then_inc(s_zs, 1)

            def copy_xt(p, blk):
                act.wait_ge(s_b, g(p, blk, 1, 1))
                act.activation(xTs, hb, ACT.Copy).then_inc(s_xt, 1)

            for p in range(5):
                def negatives(blk, h):
                    act.wait_ge(arrived[slot(1, blk)][h], uses(1, blk))
                    alone(act)
                    wait(act, s_neg, blk.at(2, h))
                    alone(act)
                    act.activation(dump, ring[:, slot(1, blk), h * HALF:(h + 1) * HALF, :], ACT.Relu, scale=-1.0,
                                   accum_out=negsum[:, bass.ds(blk.at(2, h), 1)]).then_inc(s_neg, 1)

                def step(mb, eb):
                    if eb:
                        copy_z(p, eb)
                    if p == 1 and mb:
                        negatives(mb, 0)
                        if not eb:
                            negatives(mb, 1)
                    if not eb:
                        return
                    if p == 0:
                        act.wait_ge(s_var, eb.at(2, 1))
                        act.activation(std[:, 0:4], small[:, 0:4], ACT.Sqrt).then_inc(s_std, 1)
                    for k in range(1 if p == 0 else 0, VAR[p]):
                        act.wait_ge(s_var, eb.at(VAR[p], vbase[p] + k + 1))
                        act.activation(std[:, 0:2], mv[:, :, 1], ACT.Sqrt, bias=eps).then_inc(s_std, 1)
                    if p == 1 and mb:
                        negatives(mb, 1)
                    copy_xt(p, eb)
                sweep(act, step)

            act.wait_ge(s_ex, 1)
            act.activation(e_f[:, :, :], nbits[:, :, :], ACT.Exp).then_inc(s_f, 1)

            act.wait_ge(s_flag, 1)
            any_negative = act.value_load(flag[0:1, 0:1], min_val=0, max_val=1)
            act.wait_ge(s_fp, 1)

            def powers(half, v, buf):
                for t in range(HALF):
                    tt = half * HALF + t
                    last = act.activation(pow_i[:, buf, t, :], negk[:, v % HEADS, :], ACT.Relu,
                                          bias=nbits[:, tt, v:v + 1])
                return last

            def step6(xb, wb, sb_):
                for c in range(V):
                    half, h = divmod(c, HEADS)
                    if wb:
                        if half == 0:
                            act.wait_ge(s_nk, wb.at(HEADS, h + 1))
                        if wb.c or c >= 2:
                            alone(act)
                            act.wait_ge(s_z6, wb.at(V, c - 1))
                            alone(act)
                            act.wait_ge(s_w, wb.at(V, c - 1))
                        powers(half, h, c % 2).then_inc(s_t, 1)
                    if xb and c in (ACT_CHUNKS if wb else ACT_FIRST):
                        act.wait_ge(s_mk, xb.at(2, half + 1))
                        alone(act)
                        if 2 <= c < 2 + HEADS:
                            act.wait_ge(s_tree, xb.at(V, c - 1))
                        else:
                            wait(act, s_mx, xb.at(HEADS, c - 1 if c < 2 else c - 1 - HEADS))
                        for t in range(HALF):
                            tt = half * HALF + t
                            last = act.activation(cand[:, c % 2, t, :], mask6[:, xb.c % 2, tt, :], ACT.Copy,
                                                  scale=nneg[:, tt, h:h + 1])
                        last.then_inc(s_cd, 1)
                    if wb and c % HEADS == HEADS - 1:
                        with act.If(any_negative):
                            act.wait_ge(s_c6, wb.at(V, c + 1))
                            for n in range(HEADS):
                                powers(half, HEADS + n, 0).then_inc(s_t2, 1)
                                act.wait_ge(s_c2, wb.at(V, half * HEADS + n + 1))
                            alone(act)
                    if sb_ and c == 1:
                        act.wait_ge(s_c6, sb_.at(V, V))
                        alone(act)
                        act.wait_ge(s_zo, sb_.at(16, 1))
                        alone(act)
                        bank = NUMB[sb_.c % 2]
                        act.activation(zbuf[:, :], bank[1][:, W:2 * W], ACT.Copy)
                        act.activation(stage[:, 5 * W:7 * W], bank[0][:, 0:2 * W], ACT.Copy)
                        act.activation(stage[:, 7 * W:8 * W], bank[1][:, 0:W], ACT.Copy).then_inc(s_ev, 1)
                        act.wait_ge(s_ev, sb_.at(1, 1))
                        alone(act)
                        act.dma_start(zt[bass.ds(sb_.at(1), 1), :, :].rearrange("b p c -> (b p) c"), zbuf[:, :])\
                            .then_inc(s_zo, 16)
            sweep_three(act, step6)

            act.wait_ge(s_es, B + 1)

            def step7(xb, mb, eb):
                if xb:
                    if xb.c:
                        act.wait_ge(s_b, g(5, xb, 1))
                    act.activation(xs, X[:, xb.cols(IT), :].rearrange("p i f -> p (i f)"), ACT.Copy)
                    act.activation(ys, xt_es[:, xb.cols(W)], ACT.Copy).then_inc(s_d1, 1)
                if eb:
                    for k in range(2):
                        act.wait_ge(s_cc, 5 * B + eb.at(2, k + 1))
                        alone(act)
                        act.wait_ge(s_go, eb.at(2, k + 1))
                        act.activation(gates[k][:, :, :], GATE[k][:, :, 0:2 * D], ACT.Tanh, scale=0.5)\
                            .then_inc(s_sig, 1)
                if xb:
                    if isinstance(xb.r, int) and xb.c in (0, B - 1):
                        act.wait_ge(s_z7[xb.c // (B - 1)], 16)
                    act.wait_ge(s_b, g(5, xb, 1, 1))
                    par = xb.c % 2
                    act.activation(x7[1][par], tp, ACT.Copy)
                    act.activation(h7[par], hb, ACT.Copy)
                    act.activation(x7[0][par], z7[:, xb.cols(W)], ACT.Copy).then_inc(s_xt, 1)
                if eb:
                    for k in range(2):
                        act.wait_ge(s_th, eb.at(2, k + 1))
                        act.activation(gn[k], gt[k], ACT.Tanh).then_inc(s_tn, 1)
            sweep_three(act, step7)
            act.wait_ge(s_var, vbase[5] + 1)
            act.activation(stats[:, :, 0], stats[:, :, 1], ACT.Sqrt, bias=eps).then_inc(s_std, 1)

        @block.gpsimd
        def _(pool):
            pool.wait_ge(s_nt, 1)
            pool.partition_all_reduce(negall, negtot, P, bass.bass_isa.ReduceOp.add).then_inc(s_na, 1)
            pool.wait_ge(s_f, 1)
            pool.wait_ge(s_d2, 5 * B + 1)
            for h in range(HEADS):
                hw = HW[:, :, h * D:(h + 1) * D]
                pool.tensor_tensor(hw, hw, e_f[:, :, h:h + 1].broadcast_to([P, T, D]), ALU.mult).then_inc(s_hw, 1)

            pool.wait_ge(s_flag, 1)
            any_negative = pool.value_load(flag[0:1, 0:1], min_val=0, max_val=1)

            def spread(blk, _, __):
                if not blk:
                    return
                if blk.c:
                    with pool.If(any_negative):
                        pool.wait_ge(s_t2, blk.at(V))
                        alone(pool)
                for h in range(HEADS):
                    wait(pool, s_t, blk.at(V, h + 4 - V))
                    alone(pool)
                    pool.wait_ge(s_mx, blk.at(HEADS, h + 1))
                    alone(pool)
                    pool.partition_all_reduce(negk[:, h, :], kmax[:, h, :], P, bass.bass_isa.ReduceOp.max)\
                        .then_inc(s_par, 1)
                    pool.wait_ge(s_par, blk.at(HEADS, h + 1))
                    alone(pool)
                    pool.tensor_scalar(negk[:, h, :], negk[:, h, :], -128.0 * STEP, 128.0 * (STEP * MSHIFT + 127),
                                       ALU.mult, ALU.add).then_inc(s_nk, 1)
            sweep_three(pool, spread)

        @block.vector
        def _(dve):
            q = Links(dve, s_q)
            link = q.link
            dve.memset(ones, 1.0).then_inc(s_init, 1)
            dve.memset(eps, EPS).then_inc(s_init, 1)
            dve.memset(rec, 0.0).then_inc(s_go, 2)
            dve.memset(small[:, 78:80], 0.0).then_inc(s_zo, 1)
            dve.memset(drec, 0.0).then_inc(s_d2, 1)
            dve.memset(small[:, 31:48], 0.0).then_inc(s_init, 1)
            dve.memset(small[:, 48:78], 0.0).then_inc(s_es, 1)
            dve.wait_ge(s_go, 2)
            dve.wait_ge(s_es, 1)
            dve.memset(one, 1.0).then_inc(s_init, 1)
            dve.wait_ge(s_c, 64)

            def split_rows(pair, n, dst, done):
                packed, part = pair
                r = packed[:, 3:3 + n]
                for k in range(3):
                    sel = packed[:, k:k + 1]
                    if k < 2:
                        link(dve.tensor_copy(part, r))
                        link(dve.tensor_tensor(r, r, part, ALU.subtract))
                    src = part if k < 2 else r
                    if k == 0:
                        link(dve.tensor_scalar(dst, src, sel, None, ALU.mult))
                    else:
                        st = dve.scalar_tensor_tensor(out=dst, in0=src, scalar=sel, in1=dst,
                                                      op0=ALU.mult, op1=ALU.add)
                        if k < 2:
                            link(st)
                st.then_inc(done, 1)
            split_rows(split, R_END, brow, s_init)
            dve.wait_ge(s_init, 5)
            dve.wait_ge(s_x, 16)
            dve.wait_ge(s_xc, 16)
            dve.wait_ge(s_was, 1)

            def layer_norm(y, dst, vwait):
                for i in range(IT):
                    st = dve.bn_stats(bs[:, i, :], two(y)[:, i, :])
                link(st)
                alone(dve)
                for i in range(IT):
                    st = dve.bn_aggr(mv[:, i, :], bs[:, i, :])
                st.then_inc(s_var, 1)
                dve.wait_ge(s_std, vwait)
                link(dve.reciprocal(rstd, std[:, 0:2]))
                for i in range(IT):
                    st = dve.tensor_scalar(two(dst)[:, i, :], two(y)[:, i, :], mv[:, i, 0:1], rstd[:, i:i + 1],
                                           ALU.subtract, ALU.mult)
                link(st)

            def per_row(k):
                return gb(k).rearrange("p (i f) -> p i f", i=1).broadcast_to([P, IT, D])

            def rows(buf, blk):
                return buf[:, blk.cols(IT), :]

            def f_rows(p, blk):
                return FW[:, p % 2, :].rearrange("p (t f) -> p t f", t=T)[:, blk.cols(IT), :]

            def col(ap, blk, i):
                return ap[:, bass.ds(blk.at(IT, i), 1)]

            def sums(blk, h):
                dve.wait_ge(arrived[slot(0, blk)][h], uses(0, blk))
                if h == 0 and blk.c:
                    wait(dve, s_a, blk.at(1, -1))
                dve.tensor_reduce(colsum[:, blk.c % 2, h, :],
                                  ring[:, slot(0, blk), h * HALF:(h + 1) * HALF, :].rearrange("p t c -> p c t"),
                                  AXX, ALU.add).then_inc(s_dve, 1)

            def close0(blk):
                dve.wait_ge(s_a, blk.at(1, 1))
                link(dve.tensor_tensor(sd[:, :, 0:1], E[:, :, 3 * D:3 * D + 1],
                                       dg[:, blk.cols(IT)].rearrange("p (i k) -> p i k", k=1), ALU.add))
                link(dve.tensor_scalar(sd[:, :, 1], sd[:, :, 0], 1.0, None, ALU.add))
                dve.reciprocal(rec, sd[:, :, 1]).then_inc(s_var, 1)
                dve.wait_ge(s_var, blk.at(2, 1))
                link(dve.tensor_tensor(drec, rec, dg[:, blk.cols(IT)], ALU.mult))
                for i in range(IT):
                    st = dve.tensor_scalar(two(ys)[:, i, :], E[:, i, 2 * D:3 * D], rec[:, i:i + 1], None, ALU.mult)
                link(st)
                for i in range(IT):
                    st = dve.scalar_tensor_tensor(out=two(ys)[:, i, :], in0=E[:, i, D:2 * D],
                                                  scalar=drec[:, i:i + 1], in1=two(ys)[:, i, :],
                                                  op0=ALU.mult, op1=ALU.add)
                link(st)
                link(dve.tensor_tensor(two(ys), E[:, :, 0:D], two(ys), ALU.add))
                link(dve.tensor_tensor(two(ys), f_rows(0, blk), two(ys), ALU.add))
                dve.wait_ge(s_std, blk.at(2, 1))
                link(dve.reciprocal(rows(norm, blk).rearrange("p i k -> p (i k)"), std[:, 0:4]))
                layer_norm(ys, xs, blk.at(2, 2))
                alone(dve)
                dve.tensor_copy(rows(X, blk), two(xs)).then_inc(s_d1, 1)

            def close_l(p, blk):
                dve.wait_ge(s_a, g(p, blk, 1, 1))
                for i in range(IT):
                    st = dve.scalar_tensor_tensor(out=two(ys)[:, i, :],
                                                  in0=FW[:, p % 2, bass.ds(blk.at(W, i * D), D)],
                                                  scalar=col(dg, blk, i), in1=two(tp)[:, i, :],
                                                  op0=ALU.mult, op1=ALU.add)
                link(st)
                for i in range(IT):
                    st = dve.tensor_scalar(two(ys)[:, i, :], two(ys)[:, i, :], norm[:, bass.ds(blk.at(IT, i), 1), 0],
                                           0.0, ALU.mult, ALU.max)
                link(st)
                link(dve.tensor_tensor(two(ys), two(ys), rows(res, blk), ALU.add))
                layer_norm(ys, xs, blk.at(VAR[p], vbase[p] + 1))
                link(dve.tensor_tensor(two(xs), two(xs), per_row(2 * p - 2), ALU.mult))
                if p < 3:
                    link(dve.tensor_tensor(two(xs), two(xs), per_row(2 * p - 1), ALU.add))
                    alone(dve)
                    dve.tensor_copy(rows(res, blk), two(xs)).then_inc(s_d1, 1)
                else:
                    link(dve.tensor_tensor(two(xs), two(xs), per_row(2 * p - 1), ALU.add))
                    link(dve.tensor_tensor(two(ys), two(xs), rows(X, blk), ALU.add))
                    layer_norm(ys, xs, blk.at(VAR[p], vbase[p] + 2))
                    alone(dve)
                    dve.tensor_copy(rows(X, blk), two(xs)).then_inc(s_d1, 1)

            def close4(blk):
                dve.wait_ge(s_a, g(4, blk, 1, 1))
                link(dve.tensor_scalar(diag1, dg[:, blk.cols(IT)], 1.0, None, ALU.add))
                for i in range(IT):
                    st = dve.scalar_tensor_tensor(out=two(ys)[:, i, :],
                                                  in0=FW[:, 0, bass.ds(blk.at(W, i * D), D)],
                                                  scalar=diag1[:, i:i + 1], in1=two(tp)[:, i, :],
                                                  op0=ALU.mult, op1=ALU.add)
                link(st)
                for i in range(IT):
                    st = dve.scalar_tensor_tensor(out=two(ys)[:, i, :], in0=two(ys)[:, i, :],
                                                  scalar=norm[:, bass.ds(blk.at(IT, i), 1), 1], in1=gb(6),
                                                  op0=ALU.mult, op1=ALU.add)
                link(st)
                link(dve.tensor_tensor(two(ys), two(ys), rows(X, blk), ALU.add))
                layer_norm(ys, xs, blk.at(1, vbase[4] + 1))
                alone(dve)
                dve.tensor_copy(rows(X, blk), two(xs)).then_inc(s_d1, 1)

            def operand(p, blk):
                dve.wait_ge(s_cc, g(p, blk, 1, 1))
                if p == 4:
                    alone(dve)
                    dve.tensor_copy(rows(HW, blk), E[:, :, 0:3 * D])
                    alone(dve)
                    dve.tensor_copy(rows(uraw, blk), E[:, :, 3 * D:3 * D + V]).then_inc(s_d2, 1)
                    return
                if p == 0:
                    alone(dve)
                    dve.tensor_copy(rows(res, blk), two(hc))
                for i in range(IT):
                    st = dve.tensor_scalar(FW[:, (p + 1) % 2, bass.ds(blk.at(W, i * D), D)], two(hc)[:, i, :],
                                           norm[:, bass.ds(blk.at(IT, i), 1), 1 if p == 3 else 0], None, ALU.mult)
                st.then_inc(s_d2, 1)

            close = [close0, lambda b: close_l(1, b), lambda b: close_l(2, b), lambda b: close_l(3, b), close4]
            LINKS = [2 * 11, 2 * 8, 2 * 8, 2 * 12, 2 * 7]
            for p in range(5):
                def step(mb, eb, cb):
                    if mb and p == 0:
                        sums(mb, 0)
                    if eb:
                        close[p](eb)
                    if cb:
                        operand(p, cb)
                    if mb and p == 0:
                        sums(mb, 1)
                q.sweep_three(step, LINKS[p])
                if p == 1:
                    dve.wait_ge(s_neg, 2 * B)
                    dve.tensor_reduce(negtot, negsum, AXX, ALU.add).then_inc(s_nt, 1)
                    dve.wait_ge(s_na, 1)
                    dve.tensor_scalar(flag, negall, 0.0, None, ALU.is_gt).then_inc(s_flag, 1)

            dve.wait_ge(s_d2, 5 * B + 1)
            tmp = region_m[:, 0:T * V].rearrange("p (t v) -> p t v", v=V)

            def three_parts(src, parts):
                for k in range(3):
                    link(dve.tensor_copy(parts(k), src))
                    if k < 2:
                        link(dve.tensor_tensor(src, src, parts(k), ALU.subtract))
            dve.wait_ge(s_cc, 5 * B)
            three_parts(uraw, lambda k: upos[:, :, k * V:(k + 1) * V])
            for k in range(3):
                for a in range(2):
                    st = dve.tensor_copy(uneg[:, :, k * V + a * HEADS:k * V + (a + 1) * HEADS],
                                         upos[:, :, k * V + (1 - a) * HEADS:k * V + (2 - a) * HEADS])
            st.then_inc(s_u, 1)

            def masks5(blk, h):
                dve.wait_ge(arrived[slot(5, blk)][h], uses(5, blk))
                wait(dve, s_s5, blk.at(2, h - 1))
                src = ring[:, slot(5, blk), h * HALF:(h + 1) * HALF, :]
                dve.tensor_scalar(mask5[:, h, 0], src, 0.0, None, ALU.is_gt)
                dve.tensor_scalar(mask5[:, h, 1], src, 0.0, None, ALU.is_lt).then_inc(s_m5, 1)

            def read_logits(blk):
                dve.wait_ge(s_s5, blk.at(2, 2))
                link(dve.tensor_reduce(small_e, ST[:, 0:IT * 3 * V].rearrange("p (i k v) -> p i v k", i=IT, k=3),
                                       AXX, ALU.add))
                dve.scalar_tensor_tensor(out=rows(e_f, blk), in0=small_e, scalar=ALPHA, in1=small_e,
                                         op0=ALU.mult, op1=ALU.max).then_inc(s_e5, 1)

            def step5(mb, eb, _):
                if eb:
                    read_logits(eb)
                if mb:
                    masks5(mb, 1)
                    if not (isinstance(mb.r, int) and mb.c == B - 1):
                        masks5(Block(mb.c + 1, mb.r), 0)
            masks5(Block(0), 0)
            q.sweep_three(step5, 2 * 1)

            dve.wait_ge(s_e5, B)
            dve.wait_ge(s_s5, 2 * B)
            link(dve.tensor_scalar(tmp, e_f[:, :, :], LOG2E, NMAX, ALU.mult, ALU.min))
            link(dve.tensor_scalar(tmp, tmp, -NMAX, ROUND, ALU.max, ALU.add))
            link(dve.tensor_scalar(tmp, tmp, -ROUND, None, ALU.add))
            link(dve.scalar_tensor_tensor(out=nbits[:, :, :], in0=tmp, scalar=-LN2_HI, in1=e_f[:, :, :],
                                          op0=ALU.mult, op1=ALU.add))
            dve.scalar_tensor_tensor(out=nbits[:, :, :], in0=tmp, scalar=-LN2_LO, in1=nbits[:, :, :],
                                     op0=ALU.mult, op1=ALU.add).then_inc(s_ex, 1)
            dve.wait_ge(s_f, 1)
            link(dve.tensor_scalar(nneg[:, :, :], tmp, 1.0 / STEP, 7.5 / STEP, ALU.mult, ALU.add))
            link(dve.tensor_scalar(nneg[:, :, :], nneg[:, :, :], ROUND, None, ALU.add))
            link(dve.tensor_scalar(nneg[:, :, :], nneg[:, :, :], -ROUND, None, ALU.add))
            dve.tensor_scalar(nneg[:, :, :], nneg[:, :, :], -1.0, -float(MSHIFT), ALU.mult, ALU.add)
            link(dve.tensor_scalar(nbits[:, :, :], tmp, 128.0, None, ALU.mult))
            link(dve.tensor_copy(tmp, e_f[:, :, :]))
            three_parts(tmp, lambda k: fpart[:, :, :, k])
            rpos = region_m[:, 512:512 + T * HEADS].rearrange("p (t h) -> p t h", h=HEADS)
            link(dve.reciprocal(rpos, e_f[:, :, 0:HEADS]))
            dve.tensor_tensor(e_f[:, :, HEADS:V], e_f[:, :, HEADS:V], rpos, ALU.mult).then_inc(s_fp, 1)
            dve.wait_ge(s_fp, 1)

            any_negative = dve.value_load(flag[0:1, 0:1], min_val=0, max_val=1)

            def mask(blk, half):
                dve.wait_ge(arrived[slot(6, blk)][half], uses(6, blk))
                tiles = slice(half * HALF, (half + 1) * HALF)
                dve.tensor_scalar(mask6[:, blk.c % 2, tiles, :], ring[:, slot(6, blk), tiles, :], 0.0, -1.0,
                                  ALU.is_gt, ALU.mult).then_inc(s_mk, 1)

            def own_candidates(blk, c, first):
                half, h = divmod(c, HEADS)
                if c in (ACT_FIRST if first else ACT_CHUNKS):
                    return
                dve.wait_ge(s_mk, blk.at(2, half + 1))
                for t in range(HALF):
                    tt = half * HALF + t
                    st = dve.tensor_scalar(cand[:, c % 2, t, :], mask6[:, blk.c % 2, tt, :], nneg[:, tt, h:h + 1],
                                           None, ALU.mult)
                q.mark(st)

            def first_maximum(blk, c, first):
                if first and c in ACT_FIRST:
                    dve.wait_ge(s_cd, 1 + ACT_FIRST.index(c))
                elif not first and c in ACT_CHUNKS:
                    dve.wait_ge(s_cd, blk.at(len(ACT_CHUNKS), 1 + ACT_CHUNKS.index(c)
                                             - len(ACT_CHUNKS) + len(ACT_FIRST)))
                else:
                    q.settle()
                k = cand[:, c % 2]
                m = HALF // 2
                q.mark(dve.tensor_tensor(k[:, 0:m, :], k[:, 0:m, :], k[:, HALF - m:HALF, :], ALU.max))

            def maximum(blk, c):
                half, h = divmod(c, HEADS)
                k = cand[:, c % 2]
                q.settle()
                n = HALF - HALF // 2
                while n > 2:
                    m = n // 2
                    link(dve.tensor_tensor(k[:, 0:m, :], k[:, 0:m, :], k[:, n - m:n, :], ALU.max))
                    n -= m
                if half == 0:
                    if blk.c:
                        dve.wait_ge(s_par, blk.at(HEADS, h + 1 - HEADS))
                    dve.tensor_tensor(kmax[:, h, :], k[:, 0, :], k[:, 1, :], ALU.max).then_inc(s_tree, 1)
                else:
                    dve.tensor_tensor(k[:, 0, :], k[:, 0, :], k[:, 1, :], ALU.max).then_inc(s_tree, 1)
                    dve.wait_ge(s_tree, blk.at(V, c + 1))
                    dve.tensor_tensor(kmax[:, h, :], kmax[:, h, :], k[:, 0, :], ALU.max).then_inc(s_mx, 1)

            def mask_powers(blk, c):
                tiles = slice(c // HEADS * HALF, (c // HEADS + 1) * HALF)
                dve.wait_ge(s_t, blk.at(V, c + 1))
                dve.tensor_tensor(pow_i[:, c % 2], pow_i[:, c % 2], mask6[:, blk.c % 2, tiles, :],
                                  ALU.bitwise_and).then_inc(s_tm, 1)

            def weigh(blk, c):
                tiles = slice(c // HEADS * HALF, (c // HEADS + 1) * HALF)
                dve.wait_ge(s_tm, blk.at(V, c + 1))
                if blk.c or c >= 2:
                    alone(dve)
                    dve.wait_ge(s_c6, blk.at(V, c - 1))
                dve.tensor_tensor(weight[:, c % 2], ring[:, slot(6, blk), tiles, :], pow_b[:, c % 2], ALU.mult)\
                    .then_inc(s_w, 1)

            def neg_maxima(blk):
                dve.wait_ge(arrived[slot(6, blk)][1], uses(6, blk))
                dve.wait_ge(s_tree, blk.at(V, HEADS))
                n = 0
                for t in range(T):
                    for h in range(HEADS):
                        v = HEADS + h
                        for ins in (lambda: dve.tensor_scalar(kneg, ring[:, slot(6, blk), t, :], 0.0,
                                                              nneg[:, t, v:v + 1], ALU.is_lt, ALU.mult),
                                    lambda: dve.tensor_scalar(kneg, kneg, -1.0, None, ALU.mult),
                                    lambda: dve.tensor_tensor(kmax[:, h, :], kmax[:, h, :], kneg, ALU.max)):
                            n += 1
                            ins().then_inc(s_q2, 1)
                            dve.wait_ge(s_q2, blk.at(NEG_LINKS, n))
                assert n == NEG_LINKS

            def neg_weigh(blk, half):
                dve.wait_ge(s_c6, blk.at(V, (half + 1) * HEADS))
                tiles = slice(half * HALF, (half + 1) * HALF)
                a = ring[:, slot(6, blk), tiles, :]
                for h in range(HEADS):
                    k = half * HEADS + h + 1
                    dve.wait_ge(s_t2, blk.at(V, k))
                    dve.tensor_scalar(pow_i[:, 0], pow_i[:, 0], 32512.0, None, ALU.min).then_inc(s_q3, 1)
                    dve.wait_ge(s_q3, blk.at(V, k))
                    dve.scalar_tensor_tensor(out=pow_b[:, 0], in0=a, scalar=0.0, in1=pow_b[:, 0],
                                             op0=ALU.is_lt, op1=ALU.mult).then_inc(s_tm2, 1)
                    dve.wait_ge(s_tm2, blk.at(V, k))
                    for t in range(HALF):
                        tt = half * HALF + t
                        st = dve.scalar_tensor_tensor(out=weight[:, 0, t, :], in0=a[:, t, :],
                                                      scalar=e_f[:, tt, HEADS + h:HEADS + h + 1],
                                                      in1=pow_b[:, 0, t, :], op0=ALU.mult, op1=ALU.mult)
                    st.then_inc(s_w2, 1)
                    dve.wait_ge(s_c2, blk.at(V, k))

            def sum_heads(blk):
                dve.wait_ge(s_tr, blk.at(1, 1))
                link(dve.tensor_reduce(zz, DEN[blk.c % 2][:, 0:IT * 9]
                                       .rearrange("p (i h k) -> p i h k", i=IT, h=HEADS),
                                       AXX, ALU.add))
                link(dve.tensor_scalar(zz, zz, TINY, float(HEADS), ALU.max, ALU.mult))
                link(dve.reciprocal(rz, zz))
                for h in range(HEADS):
                    for i in range(IT):
                        dst = xt_es[:, bass.ds(blk.at(W, i * D), D)]
                        src = two(hsum[h])[:, i, :]
                        if h == 0:
                            st = dve.tensor_scalar(dst, src, rz[:, i, h:h + 1], None, ALU.mult)
                        else:
                            st = dve.scalar_tensor_tensor(out=dst, in0=src, scalar=rz[:, i, h:h + 1], in1=dst,
                                                          op0=ALU.mult, op1=ALU.add)
                    if h < HEADS - 1:
                        link(st)
                st.then_inc(s_es, 1)

            def step6(xb, wb, sb_):
                for c in range(V):
                    half, h = divmod(c, HEADS)
                    if wb and not xb and c == HEADS:
                        dve.wait_ge(s_n, 32)
                        dve.memset(ones7, 1.0).then_inc(s_nr, 1)
                        split_rows(split7, R_GRU, brow7, s_nr)
                    if xb and c == 1:
                        mask(xb, 1)
                    if xb and c == V - 1 and not (isinstance(xb.r, int) and xb.c == B - 1):
                        mask(Block(xb.c + 1, xb.r), 0)
                    if xb and c == HEADS:
                        with dve.If(any_negative):
                            neg_maxima(xb)
                            alone(dve)
                    if xb:
                        own_candidates(xb, c, not wb)
                    if wb:
                        mask_powers(wb, c)
                    if xb:
                        first_maximum(xb, c, not wb)
                    if wb:
                        weigh(wb, c)
                    if xb:
                        maximum(xb, c)
                    if sb_ and c == 3:
                        sum_heads(sb_)
                    if wb and h == HEADS - 1:
                        with dve.If(any_negative):
                            neg_weigh(wb, half)
                            alone(dve)
                        dve.wait_ge(s_dve, wb.at(2, 2 * B + half))
                        alone(dve)
                        dve.memset(cell, 0.0).then_inc(s_dve, 1)
            mask(Block(0), 0)
            q.sweep_three(step6, 2 * (V * 3 + V - len(ACT_CHUNKS) + 5))


            def gate_sum(k, n):
                dve.wait_ge(s_sig, n)
                link(dve.scalar_tensor_tensor(out=two(gt[k]), in0=gates[k][:, :, 0:D], scalar=1.0,
                                              in1=GATE[k][:, :, 3 * D:4 * D], op0=ALU.add, op1=ALU.mult))
                dve.scalar_tensor_tensor(out=two(gt[k]), in0=two(gt[k]), scalar=0.5,
                                         in1=GATE[k][:, :, 2 * D:3 * D], op0=ALU.mult, op1=ALU.add).then_inc(s_th, 1)

            def gru_result(k, n, blk, dst):
                dve.wait_ge(s_tn, n)
                link(dve.tensor_tensor(two(gt[k]), rows(X, blk), two(gn[k]), ALU.subtract))
                link(dve.scalar_tensor_tensor(out=two(gt[k]), in0=gates[k][:, :, D:2 * D], scalar=1.0,
                                              in1=two(gt[k]), op0=ALU.add, op1=ALU.mult))
                dve.scalar_tensor_tensor(out=two(dst), in0=two(gt[k]), scalar=0.5, in1=two(gn[k]),
                                         op0=ALU.mult, op1=ALU.add).then_inc(s_go, 1)

            def step7(_, blk):
                if not blk:
                    return
                for k in range(2):
                    gate_sum(k, blk.at(2, k + 1))
                for k in range(2):
                    gru_result(k, blk.at(2, k + 1), blk, (edge_rows, gt[1])[k])
                dve.wait_ge(s_go, blk.at(2, 4))
                link(dve.tensor_tensor(gt[1], gt[1], edge_rows, ALU.add))
                for i in range(IT):
                    xi = X[:, bass.ds(blk.at(IT, i), 1), :].rearrange("p i f -> p (i f)")
                    st = dve.scalar_tensor_tensor(out=xi, in0=two(gt[1])[:, i, :], scalar=col(dg, blk, i), in1=xi,
                                                  op0=ALU.mult, op1=ALU.add)
                link(st)
                alone(dve)
                for i in range(IT):
                    xi = X[:, bass.ds(blk.at(IT, i), 1), :].rearrange("p i f -> p (i f)")
                    st = dve.bn_stats(bs[:, i, :], xi)
                link(st)
                alone(dve)
                for i in range(IT):
                    st = dve.bn_aggr(mv[:, i, :], bs[:, i, :])
                link(st)
                alone(dve)
                link(dve.tensor_copy(rows(stats, blk), mv))
            q.sweep(step7, 2 * 11)
            dve.tensor_copy(e_f[:, :, 0], stats[:, :, 0]).then_inc(s_var, 1)
            dve.wait_ge(s_std, vbase[5] + 1)
            link(dve.reciprocal(e_f[:, :, 1], stats[:, :, 0]))
            for t in range(T):
                st = dve.tensor_scalar(res[:, t, :], X[:, t, :], e_f[:, t, 0:1], e_f[:, t, 1:2],
                                       ALU.subtract, ALU.mult)
                if t in (HALF - 1, T - 1):
                    st.then_inc(s_fin, 1)


def kernel(x, adj, L0_gnn_W, L1_gnn_W1, L1_gnn_b1, L1_gnn_W2, L1_gnn_b2, L1_gnn_W3, L1_gnn_b3,
           L1_gnn_g1, L1_gnn_be1, L1_gnn_g2, L1_gnn_be2, L1_gnn_g3, L1_gnn_be3,
           L2_gnn_weight, L2_gnn_bias, L3_gnn_gat_W, L3_gnn_gat_a,
           L3_gnn_edge_Wih, L3_gnn_edge_Whh, L3_gnn_edge_bih, L3_gnn_edge_bhh,
           L3_gnn_node_Wih, L3_gnn_node_Whh, L3_gnn_node_bih, L3_gnn_node_bhh):
    import numpy as np
    import concourse.bacc as bacc
    from concourse.bass_utils import run_bass_kernel_spmd

    def arr(a):
        return np.asarray(a)

    x, adj = arr(x), arr(adj)
    NP_ = T * P
    off = np.zeros((NP_, NP_), np.float32)
    off[:N, :N] = adj.T
    node = np.arange(NP_)
    off[node, node] = 0.0
    dgn = np.ones(NP_, np.float32)
    dgn[:N] = adj[np.arange(N), np.arange(N)]
    xp = np.zeros((NP_, D), np.float32)
    xp[:N] = x
    a = arr(L3_gnn_gat_a)[:, :, 0].reshape(HEADS, 2, D)
    gw = arr(L3_gnn_gat_W)

    def wide(v):
        return np.broadcast_to(arr(v), (P, D))
    w0 = arr(L0_gnn_W)
    consts = np.concatenate(
        [w0[:, :D].T, w0[:, D:].T, arr(L1_gnn_W1), arr(L1_gnn_W2), arr(L1_gnn_W3), arr(L2_gnn_weight),
         gw.transpose(1, 0, 2).reshape(D, -1), gw.transpose(2, 0, 1).reshape(D, -1),
         a.transpose(2, 0, 1).reshape(D, V)]
        + [wide(v) for v in (L1_gnn_g1, L1_gnn_be1, L1_gnn_g2, L1_gnn_be2, L1_gnn_g3, L1_gnn_be3, L2_gnn_bias)],
        axis=1)
    none = np.zeros(D, np.float32)

    def bias_rows(x_side, h_side):
        pair = [x_side, h_side]
        return np.stack([np.concatenate([np.eye(3, dtype=np.float32)[k // 2], *pair[k % 2]]) for k in range(BK)])
    rows = bias_rows([arr(v) for v in (L1_gnn_b1, L1_gnn_b2, L1_gnn_b3)], [none] * 3)
    bih = [arr(v) for v in (L3_gnn_edge_bih, L3_gnn_node_bih)]
    bhh = [arr(v) for v in (L3_gnn_edge_bhh, L3_gnn_node_bhh)]
    arrays = {
        "adjt": off.reshape(T, P, B, W).transpose(2, 1, 0, 3),
        "diag": dgn.reshape(T, P).T,
        "xrow": xp.reshape(T, P, D).transpose(1, 0, 2).reshape(P, T * D),
        "xcol": xp.T,
        "consts": consts,
        "rows": rows,
        "gru": np.stack([np.stack([arr(i).T, arr(h).T], axis=1) for i, h in
                         ((L3_gnn_edge_Wih, L3_gnn_edge_Whh), (L3_gnn_node_Wih, L3_gnn_node_Whh))], axis=1),
        "gru_rows": bias_rows([v for b in bih for v in (b, none)],
                              [v for b in bhh for v in (b[:2 * D], none, b[2 * D:])]),
        "ident": np.eye(P, dtype=np.float32),
    }
    arrays = {k: np.ascontiguousarray(v) for k, v in arrays.items()}
    nc = bacc.Bacc("TRN2", target_bir_lowering=False, num_devices=1)
    args = {k: nc.dram_tensor(k + "_dram", v.shape, F32, kind="ExternalInput").ap() for k, v in arrays.items()}
    out = nc.dram_tensor("out_dram", (NP_, D), F32, kind="ExternalOutput").ap()
    zt = nc.dram_tensor("zt_dram", (B, P, W), F32, kind="Internal").ap()
    build(nc, zt=zt, out=out, **args)
    r = run_bass_kernel_spmd(nc, [{k + "_dram": v for k, v in arrays.items()}], core_ids=[0])
    return r.results[0]["out_dram"][:N]
```
